# Optimizing a Trainium2 kernel written in Bass

```python
import numpy as np
import jax
import jax.numpy as jnp

def _softmax(x, axis=-1):
    return jax.nn.softmax(x, axis=axis)

def _gelu(x):
    return jax.nn.gelu(x, approximate=True)

def _silu(x):
    return jax.nn.silu(x)

def _sigmoid(x):
    return jax.nn.sigmoid(x)

def _layernorm(x, axis=-1, eps=1e-05):
    m = jnp.mean(x, axis=axis, keepdims=True)
    v = jnp.var(x, axis=axis, keepdims=True)
    return (x - m) / jnp.sqrt(v + eps)

def _scatter_add(tgt, idx, src, axis=0):
    return tgt.at[idx].add(src)

def _segment_sum(src, seg, n):
    return jax.ops.segment_sum(src, seg, n)
kernel_name = 'mk_adj_resnorm_d1_adj_r2_4d28b4'

def setup_inputs(seed: int=0):
    np.random.seed(seed)
    _w = jnp.asarray

    def _rec_inputs():
        import jax
        import jax.numpy as jnp
        _gk = jax.random.key(seed)
        x = -0.0002928 + 1 * jax.random.normal(jax.random.fold_in(_gk, 1), (8, 1024, 256), jnp.float32)
        _a = jax.random.bernoulli(jax.random.fold_in(_gk, 2), 0.0078125, (8, 1024, 1024))
        adj = _a
        return (x, adj)
    x, adj = _rec_inputs()

    def _L0_gnn_setup():
        import jax, jax.numpy as jnp
        import numpy as np
        QUERY_DIM = 256
        HEADS = 4
        DIM_HEAD = 64
        INNER = HEADS * DIM_HEAD
        B, N = (4, 1024)
        key = jax.random.key(seed)
        ks = jax.random.split(key, 6)
        s = 1.0 / np.sqrt(QUERY_DIM)
        x = jax.random.normal(ks[0], (B, N, QUERY_DIM), dtype=jnp.float32)
        adjacency_mask = jax.random.randint(ks[1], (B, N, N), 0, 2) > 0
        Wq = jax.random.normal(ks[2], (QUERY_DIM, INNER), dtype=jnp.float32) * s
        Wk = jax.random.normal(ks[3], (QUERY_DIM, INNER), dtype=jnp.float32) * s
        Wv = jax.random.normal(ks[4], (QUERY_DIM, INNER), dtype=jnp.float32) * s
        Wo = jax.random.normal(ks[5], (INNER, QUERY_DIM), dtype=jnp.float32) * (1.0 / np.sqrt(INNER))
        bo = jnp.zeros((QUERY_DIM,), dtype=jnp.float32)
        return {'x': x, 'adjacency_mask': adjacency_mask, 'Wq': Wq, 'Wk': Wk, 'Wv': Wv, 'Wo': Wo, 'bo': bo}
    _L0_gnn_all = _L0_gnn_setup()
    _L0_gnn_in = {k: v for k, v in _L0_gnn_all.items() if k in ('Wq', 'Wk', 'Wv', 'Wo', 'bo')}
    del _L0_gnn_all
    return {'x': x, 'adj': adj, 'L0_gnn_Wq': _L0_gnn_in['Wq'], 'L0_gnn_Wk': _L0_gnn_in['Wk'], 'L0_gnn_Wv': _L0_gnn_in['Wv'], 'L0_gnn_Wo': _L0_gnn_in['Wo'], 'L0_gnn_bo': _L0_gnn_in['bo']}

def reference(x, adj, L0_gnn_Wq, L0_gnn_Wk, L0_gnn_Wv, L0_gnn_Wo, L0_gnn_bo):
    import jax
    import jax.numpy as jnp

    def _L0_gnn_ref(x, adjacency_mask, Wq, Wk, Wv, Wo, bo):
        import jax, jax.numpy as jnp
        import numpy as np
        QUERY_DIM = 256
        HEADS = 4
        DIM_HEAD = 64
        INNER = HEADS * DIM_HEAD
        B, N = (4, 1024)
        scale = DIM_HEAD ** (-0.5)

        def split_heads(t):
            b, n, _ = t.shape
            return t.reshape(b, n, HEADS, DIM_HEAD).transpose(0, 2, 1, 3)
        q = split_heads(x @ Wq)
        k = split_heads(x @ Wk)
        v = split_heads(x @ Wv)
        sim = jnp.einsum('bhid,bhjd->bhij', q, k) * scale
        neg = -jnp.finfo(sim.dtype).max
        sim = jnp.where(adjacency_mask[:, None, :, :], sim, neg)
        attn = jax.nn.softmax(sim, axis=-1)
        out = jnp.einsum('bhij,bhjd->bhid', attn, v)
        out = out.transpose(0, 2, 1, 3).reshape(x.shape[0], x.shape[1], INNER)
        return out @ Wo + bo
    x = _layernorm(x + _L0_gnn_ref(x, adj, L0_gnn_Wq, L0_gnn_Wk, L0_gnn_Wv, L0_gnn_Wo, L0_gnn_bo), axis=-1)
    return x

_drawn_inputs = setup_inputs


def setup_inputs(seed=0):
    import zlib

    import numpy as np

    out = dict(_drawn_inputs(seed))
    spreads = {'L0_gnn_bo': (0.0, 0.1)}
    factors = {}
    for name, (base, spread) in spreads.items():
        noise = np.random.default_rng([zlib.crc32(name.encode()), seed]).standard_normal(out[name].shape)
        drawn = base * np.exp(spread * noise) if base else spread * noise
        out[name] = jnp.asarray(drawn.astype(out[name].dtype))
    for name, factor in factors.items():
        out[name] = (out[name] * factor).astype(out[name].dtype)
    return out
```

```python
from contextlib import ExitStack

import concourse.bass as bass
from concourse import mybir

F32 = mybir.dt.float32
F32R = mybir.dt.float32r
BF16 = mybir.dt.bfloat16
U8 = mybir.dt.uint8
ALU = mybir.AluOpType
ACT = mybir.ActivationFunctionType
AX_X = mybir.AxisListType.X

P = 128
HALF = 512
BIG = 2.0 ** 100
EPS = 1e-5


def slot_plan(pp):
    plan = [[[] for _ in range(6)] for _ in range(8)]
    maxima = [("max", (i, h, f)) for i in range(8) for h in range(2) for f in range(2)]
    for s, places in MAXIMA:
        for at in places:
            plan[s][at].append(maxima.pop(0))
    assert not maxima
    for kind, idx, s, at in MORE[pp]:
        plan[s][at].append((kind, idx))
    return plan


MAXIMA = [(1, (2, 3, 4, 5))] + [(s, (1, 2, 3, 4, 5)) for s in range(2, 7)] + [(7, (1, 2, 3))]
MORE = [
    [("v", 3, 1, 0), ("l", 0, 2, 5), ("l", 1, 3, 0), ("prj", 0, 4, 0), ("prj", 1, 5, 0), ("prj", 2, 6, 0),
     ("prj", 3, 7, 0), ("mt", 0, 7, 5), ("mt", 1, 7, 5), ("o", 0, 6, 5), ("o", 1, 7, 2)],
    [("o", 2, 0, 0), ("o", 3, 0, 0), ("fin", 0, 1, 0), ("l", 0, 2, 5), ("l", 1, 3, 0), ("v", 0, 3, 2), ("prj", 0, 4, 0),
     ("prj", 1, 5, 0), ("prj", 2, 6, 0), ("prj", 3, 7, 0), ("mt", 0, 7, 5), ("mt", 1, 7, 5), ("v", 1, 5, 2), ("v", 2, 7, 2)],
]
PARTS = [["a0", "s00", "s01", "a1", "s10", "s11"]] + [["s00", "s01", "a0", "s10", "s11", "a1"]] * 7
PLANS = [slot_plan(0), slot_plan(1)]
MASKED_BY_PE = [(0, 1), (1, 0)]
MASKED_BY_DVE = [(h, f) for h in range(2) for f in range(2) if (h, f) not in MASKED_BY_PE]


class AuxBanks:

    def __init__(self, banks):
        self.banks, self.n, self.held_by = banks, 0, [None] * len(banks)

    def next(self):
        self.n += 1
        return self.banks[(self.n - 1) % len(self.banks)]

    def take(self, item):
        k = self.n % len(self.banks)
        before, self.held_by[k] = self.held_by[k], item
        return self.next(), before

    def enter_loop(self, b):
        self.held_by = [(kind, idx, b - 1, pp) for kind, idx, _, pp in self.held_by]


def masked_attention_residual_norm(nc, xt, x, adj, adjt, wq, wk, wv, wo, bo, out):
    B, N, D = x.shape
    H = 4
    DH = D // H
    PAIRS = H // 2
    T = N // P
    KT = D // P
    SCALE = DH ** -0.5
    RING = 4
    assert T == 8 and KT == 2 and DH == 64 and PAIRS == 2 and N == 2 * HALF

    xt_v = xt.rearrange("b (k p) n -> b p k n", p=P)
    x_v = x.rearrange("b (t p) d -> b p t d", p=P)
    out_v = out.rearrange("b (t p) d -> b p t d", p=P)
    adj_v = adj.rearrange("b (c t p) n -> b c p t n", p=P, t=2)
    adjt_v = adjt.rearrange("b (c t p) n -> b c p t n", p=P, t=2)
    w_v = [w.rearrange("(k p) n -> p k n", p=P) for w in (wq, wk, wv, wo)]

    with ExitStack() as ctx:
        def sb(name, shape, dt=F32):
            return ctx.enter_context(nc.sbuf_tensor(name, shape, dt))

        def psum(name, shape):
            return ctx.enter_context(nc.psum_tensor(name, shape, F32))

        def sem(name):
            return ctx.enter_context(nc.semaphore(name))

        w_sb = [sb(f"w{n}", [P, KT, D]) for n in ("q", "k", "v", "o")]
        bias_row = sb("bias_row", [P, D])
        ident = sb("ident", [P, P])
        ident0 = sb("ident0", [P, P])
        ident_bf = sb("ident_bf", [P, P], BF16)
        ones = sb("ones", [P, DH])
        eps = sb("eps", [P, 1])
        two = sb("two", [P, 1])
        xt_sb = sb("xt_sb", [P, KT, N])
        adj_u8 = [sb(f"adj_u8_{i}", [P, 2, N], U8) for i in range(2)]
        mask_n = sb("mask_n", [P, T, N], BF16)
        mask_t = sb("mask_t", [P, T, N], BF16)
        q1 = [sb(f"q1_{i}", [P, 2, N], F32R) for i in range(2)]
        k1 = [sb(f"k1_{i}", [P, 2, N], F32R) for i in range(2)]
        q2 = [sb(f"q2_{i}", [P, 2, N], F32R) for i in range(2)]
        k2 = [sb(f"k2_{i}", [P, 2, N], F32R) for i in range(2)]
        hi = [sb("q_hi", [P, N], F32R), sb("k_hi", [P, N], F32R)]
        lo = [sb("q_lo", [P, N], F32R), sb("k_lo", [P, N], F32R)]
        v_sb = sb("v_sb", [P, T, D])
        probs = [sb(f"probs{i}", [P, 2, N]) for i in range(RING)]
        psums = sb("psums", [P, 2, N])
        ot = sb("ot", [P, PAIRS, N])
        sums = sb("sums", [P, N])
        rsum = sb("rsum", [P, N])
        y = sb("y", [P, T, D])
        mx = sb("mx", [P, T, 2, 2])
        m = sb("m", [P, T, 2])
        stats = sb("stats", [P, T, 6])
        mv = sb("mv", [P, T, 2])
        std = sb("std", [P, T])
        rstd = sb("rstd", [P, T])

        st = [[psum(f"st{h}{f}", [P, HALF]) for f in range(2)] for h in range(2)]
        ot_ps = psum("ot_ps", [P, 2, HALF])
        aux = [psum(f"aux{i}", [P, HALF]) for i in range(2)]

        names = ("w_in bias_in xt_in adj_in0 adj_in1 x_in out_st op_in w_pool apart ident_set const_set sel_set "
                 "st_full pv_done max_full mt_full prj_full v_full l_full o_full "
                 "masked max_red m_done lo_done r_done n_done l_copied r_near newton y_sum y_stat y_aggr y_rstd y_done "
                 "p_ready hi_done mrow_done v_ready ot_raw conv std_done sum_done xb_done")
        S = {n: sem(n) for n in names.split()}
        adj_in = [S["adj_in0"], S["adj_in1"]]

        def n_unit(s, j, h, f):
            return s * 32 + (4 * j + 2 * h + f + 1)

        def n_masked(s, j, h, f):
            per_tile = len(MASKED_BY_DVE)
            return s * (T * per_tile) + (j * per_tile + MASKED_BY_DVE.index((h, f)) + 1)

        def n_tile(s, j):
            return s * T + (j + 1)

        def n_max(s, i, h, f):
            return s * 32 + (4 * i + 2 * h + f + 1)

        def n_half(s, f):
            return s * 2 + (f + 1)

        def n_row(s, f):
            return s * 4 + (2 * f + 2)

        def n_prj(s, k):
            return s * 4 + (k + 1)

        def n_four(b, c):
            return b * 4 + (c + 1)

        def n_conv(b, c, transposed):
            return b * 8 + (4 * transposed + c + 1)

        def reader_of(kind, idx, b, pp):
            s = b * 2 + pp
            if kind == "max":
                return S["max_red"], n_max(s + 1, *idx)
            if kind == "mt":
                return S["mrow_done"], n_row(s + 1, idx)
            if kind == "prj":
                return S["lo_done"], n_prj(s + 2, idx)
            if kind == "v":
                return S["v_ready"], n_four(b + 1 if pp else b, idx)
            if kind == "l":
                return S["l_copied"], n_half(s - 1, idx)
            return S["y_sum"], n_four(b - 1, idx)

        def present(kind, idx, b, pp, first, last):
            if kind in ("max", "mt"):
                return not (last and pp == 1)
            if kind == "prj":
                return not last
            if kind == "v":
                return not (last and pp == 1)
            if kind == "l":
                return not (first and pp == 0)
            return not first

        def drive(engine, body, banks=None):
            body(0, True, False)
            with engine.Fori(1, B - 1) as b:
                if banks is not None:
                    banks.enter_loop(b)
                body(b, False, False)
            if banks is not None:
                banks.enter_loop(B - 1)
            body(B - 1, False, True)

        def wait_apart(engine, semaphore, value):
            engine.wait_ge(semaphore, value)
            if not isinstance(value, int):
                engine.sem_inc(S["apart"], 1)

        block = ctx.enter_context(nc.Block())

        @block.sync
        def _(sp):
            def load_adj(b, c, transposed):
                g = 4 * transposed + c
                if not (isinstance(b, int) and b == 0 and g < 2):
                    wait_apart(sp, S["conv"], b * 8 + (g - 1))
                src = (adjt_v if transposed else adj_v)[b, c]
                sp.dma_start(adj_u8[g % 2][:], src).then_inc(adj_in[g % 2], 16)

            def load_ops(s, par):
                sp.wait_ge(S["hi_done"], n_prj(s, 3))
                sp.wait_ge(S["lo_done"], n_prj(s, 3))
                if not isinstance(s, int) or s >= 2:
                    sp.wait_ge(S["st_full"], n_unit(s - 2, T - 1, 1, 1))
                lohalf, hihalf = slice(0, DH), slice(DH, P)
                for src, dst in (
                    (hi[0][lohalf, :], q1[par][lohalf, 0]), (lo[0][lohalf, :], q1[par][hihalf, 0]),
                    (hi[1][lohalf, :], k1[par][lohalf, 0]), (hi[1][lohalf, :], k1[par][hihalf, 0]),
                    (lo[0][hihalf, :], q1[par][lohalf, 1]), (hi[0][hihalf, :], q1[par][hihalf, 1]),
                    (hi[1][hihalf, :], k1[par][lohalf, 1]), (hi[1][hihalf, :], k1[par][hihalf, 1]),
                    (hi[0][lohalf, :], q2[par][lohalf, 0]), (lo[1][lohalf, :], k2[par][lohalf, 0]),
                    (hi[0][hihalf, :], q2[par][hihalf, 1]), (lo[1][hihalf, :], k2[par][hihalf, 1]),
                ):
                    sp.dma_start(dst.bitcast(F32), src.bitcast(F32)).then_inc(S["op_in"], 16)

            def store(b):
                for f in range(2):
                    wait_apart(sp, S["y_done"], b * T + (T // 2) * (f + 1))
                    h = slice(f * T // 2, (f + 1) * T // 2)
                    sp.dma_start(out_v[b][:, h], y[:, h]).then_inc(S["out_st"], 16)

            def body(b, first, last):
                if not last:
                    wait_apart(sp, S["v_full"], n_four(b, 3))
                    sp.dma_start(xt_sb[:], xt_v[b + 1]).then_inc(S["xt_in"], 16)
                    for c in range(4):
                        load_adj(b + 1, c, False)
                load_ops_next = not last
                if load_ops_next:
                    load_ops(b * 2 + 2, 0)
                if not first:
                    store(b - 1)
                    wait_apart(sp, S["out_st"], b * 32)
                sp.dma_start(y[:], x_v[b]).then_inc(S["x_in"], 16)
                if not last:
                    for c in range(4):
                        load_adj(b + 1, c, True)
                    load_ops(b * 2 + 3, 1)

            sp.dma_start(xt_sb[:], xt_v[0]).then_inc(S["xt_in"], 16)
            for n in range(4):
                sp.dma_start(w_sb[n][:], w_v[n]).then_inc(S["w_in"], 16)
            sp.dma_start(bias_row[:], bo.rearrange("(a d) -> a d", a=1).to_broadcast([P, D])).then_inc(S["bias_in"], 16)
            for c in range(4):
                load_adj(0, c, False)
            load_ops(0, 0)
            for c in range(4):
                load_adj(0, c, True)
            load_ops(1, 1)
            drive(nc.sync, body)
            store(B - 1)
            sp.wait_ge(S["out_st"], B * 32)

        @block.tensor
        def _(pe):
            banks = AuxBanks(aux)

            def scores(s, pp, j, h, f):
                if h == 0 and f == 0 and j == 0:
                    pe.wait_ge(S["mrow_done"], n_row(s, 1))
                if not (isinstance(s, int) and s == 0 and j == 0):
                    pe.wait_ge(S["p_ready"], n_unit(s, j, h, f) - 4)
                js, fs = slice(j * P, (j + 1) * P), slice(f * HALF, (f + 1) * HALF)
                by_dve = (h, f) in MASKED_BY_DVE
                nc.tensor.matmul(st[h][f][:], k1[pp][:, h, js], q1[pp][:, h, fs], start=True, stop=False)
                done = nc.tensor.matmul(st[h][f][:], k2[pp][:, h, js], q2[pp][:, h, fs], start=False, stop=by_dve)
                if not by_dve:
                    done = nc.tensor.matmul(st[h][f][:], ident_bf[:], mask_t[:, j, fs], start=False, stop=True)
                done.then_inc(S["st_full"], 1)

            def attend(s, pp, j, f):
                pe.wait_ge(S["p_ready"], n_unit(s, j, 1, f))
                if f == 0:
                    if j % 2 == 0 and pp == 0:
                        pe.wait_ge(S["v_ready"], s * 2 + (j // 2 + 1))
                    if j == 0 and not (isinstance(s, int) and s == 0):
                        pe.wait_ge(S["ot_raw"], n_half(s - 1, 1))
                fs = slice(f * HALF, (f + 1) * HALF)
                for h in range(2):
                    c = (pp * 2 + h) * DH
                    last = nc.tensor.matmul(ot_ps[h * DH:(h + 1) * DH, f], v_sb[:, j, c:c + DH],
                                            probs[j % RING][:, h, fs], start=(j == 0), stop=(j == T - 1))
                if f == 1:
                    last.then_inc(S["pv_done"], 1)

            def item(kind, idx, b, pp):
                s = b * 2 + pp
                bank, before = banks.take((kind, idx, b, pp))
                if before is not None:
                    pe.wait_ge(*reader_of(*before))
                if kind == "max":
                    i, h, f = idx
                    par = (pp + 1) % 2
                    if i == 0 and h == 0 and f == 0:
                        pe.wait_ge(S["op_in"], s * 192 + 384)
                    nc.tensor.matmul(bank[:], q1[par][:, h, i * P:(i + 1) * P], k1[par][:, h, f * HALF:(f + 1) * HALF],
                                     start=True, stop=True).then_inc(S["max_full"], 1)
                elif kind == "mt":
                    if idx == 0:
                        pe.wait_ge(S["m_done"], s + 2)
                    for t in range(4):
                        last = nc.tensor.transpose(bank[0:2, t * P:(t + 1) * P], m[:, 4 * idx + t, :], ident[:])
                    last.then_inc(S["mt_full"], 1)
                elif kind == "prj":
                    which, f = idx // 2, idx % 2
                    par = pp
                    if idx == 0 and par == 0:
                        pe.wait_ge(S["xt_in"], b * 16 + 32)
                    for k in range(KT):
                        last = nc.tensor.matmul(bank[:], w_sb[which][:, k, par * P:(par + 1) * P],
                                                xt_sb[:, k, f * HALF:(f + 1) * HALF], start=(k == 0), stop=(k == KT - 1))
                    last.then_inc(S["prj_full"], 1)
                elif kind == "v":
                    for t in range(2):
                        j = 2 * idx + t
                        for k in range(KT):
                            last = nc.tensor.matmul(bank[:, t * D:(t + 1) * D], xt_sb[:, k, j * P:(j + 1) * P],
                                                    w_sb[2][:, k, :], start=(k == 0), stop=(k == KT - 1))
                    last.then_inc(S["v_full"], 1)
                elif kind == "l":
                    if idx == 0:
                        pe.wait_ge(S["sum_done"], (s - 1) * (T - 1) + (T - 1))
                    for h in range(2):
                        last = nc.tensor.matmul(bank[h * DH:(h + 1) * DH, :], ones[:], psums[:, h, idx * HALF:(idx + 1) * HALF],
                                                start=True, stop=True)
                    last.then_inc(S["l_full"], 1)
                else:
                    if idx == 0:
                        pe.wait_ge(S["n_done"], b * 2)
                    for t in range(2):
                        i = 2 * idx + t
                        for k in range(KT):
                            last = nc.tensor.matmul(bank[:, t * D:(t + 1) * D], ot[:, k, i * P:(i + 1) * P],
                                                    w_sb[3][:, k, :], start=(k == 0), stop=(k == KT - 1))
                    last.then_inc(S["o_full"], 1)

            def body(b, first, last):
                for pp in range(2):
                    s = b * 2 + pp
                    for j in range(T):
                        for g, part in enumerate(PARTS[j]):
                            if part == "s00" and pp == 0 and j % 2 == 0:
                                pe.wait_ge(S["conv"], n_conv(b, j // 2, True))
                            if part[0] == "s":
                                scores(s, pp, j, int(part[1]), int(part[2]))
                            elif j > 0:
                                attend(s, pp, j - 1, int(part[1]))
                            elif not (first and pp == 0):
                                attend(s - 1, 1 - pp, T - 1, int(part[1]))
                            for kind, idx in PLANS[pp][j][g]:
                                if kind != "fin" and present(kind, idx, b, pp, first, last):
                                    item(kind, idx, b, pp)

            pe.wait_ge(S["w_in"], 64)
            pe.wait_ge(S["xt_in"], 16)
            pe.wait_ge(S["const_set"], 3)
            for k in range(4):
                item("prj", k, -1, 0)
            for c in range(3):
                item("v", c, -1, 1)
            for k in range(4):
                item("prj", k, -1, 1)
            for i in range(T):
                for h in range(2):
                    for f in range(2):
                        item("max", (i, h, f), -1, 1)
            for f in range(2):
                item("mt", f, -1, 1)
            pe.wait_ge(S["sel_set"], 9)
            drive(nc.tensor, body, banks)
            attend(2 * B - 1, 1, T - 1, 0)
            attend(2 * B - 1, 1, T - 1, 1)
            for f in range(2):
                item("l", f, B, 0)
            for c in range(4):
                item("o", c, B, 0)

        @block.vector
        def _(dve):
            banks = AuxBanks(aux)

            def mask(s, j, h, f):
                dve.wait_ge(S["st_full"], n_unit(s, j, h, f))
                nc.vector.tensor_tensor(out=st[h][f][:], in0=st[h][f][:], in1=mask_t[:, j, f * HALF:(f + 1) * HALF],
                                        op=ALU.add).then_inc(S["masked"], 1)

            def norm(b, c):
                for t in range(2 * c, 2 * c + 2):
                    nc.vector.bn_stats(stats[:, t, :], y[:, t, :]).then_inc(S["y_stat"], 1)

            def finish(b):
                wait_apart(dve, S["y_stat"], b * T + T)
                for t in range(T):
                    nc.vector.bn_aggr(mv[:, t, :], stats[:, t, :]).then_inc(S["y_aggr"], 1)
                dve.wait_ge(S["std_done"], b + 1)
                nc.vector.reciprocal(rstd[:], std[:]).then_inc(S["y_rstd"], 1)
                dve.wait_ge(S["y_rstd"], b + 1)
                for t in range(T):
                    nc.vector.tensor_scalar(y[:, t, :], y[:, t, :], mv[:, t, 0:1], rstd[:, t:t + 1],
                                            ALU.subtract, ALU.mult).then_inc(S["y_done"], 1)

            def item(kind, idx, b, pp):
                s = b * 2 + pp
                bank = banks.next()
                if kind == "max":
                    i, h, f = idx
                    if h == 0 and f == 0 and i % 2 == 0:
                        dve.wait_ge(S["conv"], n_conv(b + pp, i // 2, False))
                    if i == 0 and h == 0 and f == 0 and not (isinstance(s, int) and s < 0):
                        dve.wait_ge(S["m_done"], s + 1)
                    wait_apart(dve, S["max_full"], n_max(s + 1, i, h, f))
                    nc.vector.tensor_tensor_reduce(
                        out=bank[:], in0=bank[:], in1=mask_n[:, i, f * HALF:(f + 1) * HALF], scale=1.0,
                        scalar=-3.0e38, op0=ALU.add, op1=ALU.max, accum_out=mx[:, i, h, f:f + 1]).then_inc(S["max_red"], 1)
                    if i == T - 1 and h == 1 and f == 1:
                        dve.wait_ge(S["max_red"], n_max(s + 1, i, h, f))
                        if not (isinstance(s, int) and s < 0):
                            dve.wait_ge(S["mt_full"], n_half(s, 1))
                        nc.vector.tensor_reduce(m[:], mx[:], AX_X, ALU.max).then_inc(S["m_done"], 1)
                elif kind == "prj":
                    which, f = idx // 2, idx % 2
                    fs = slice(f * HALF, (f + 1) * HALF)
                    if idx == 0 and not (isinstance(s, int) and s < -1):
                        dve.wait_ge(S["op_in"], s * 192 + 384)
                    dve.wait_ge(S["hi_done"], n_prj(s + 2, idx))
                    nc.vector.tensor_tensor(out=lo[which][:, fs], in0=bank[:], in1=hi[which][:, fs].bitcast(F32),
                                            op=ALU.subtract).then_inc(S["lo_done"], 1)
                elif kind == "o":
                    if idx == 0:
                        dve.wait_ge(S["xb_done"], b)
                    dve.wait_ge(S["o_full"], n_four(b - 1, idx))
                    ys = y[:, 2 * idx:2 * idx + 2, :]
                    nc.vector.tensor_tensor(out=ys, in0=bank[:].rearrange("p (t d) -> p t d", t=2), in1=ys,
                                            op=ALU.add).then_inc(S["y_sum"], 1)
                    dve.wait_ge(S["y_sum"], n_four(b - 1, idx))
                    norm(b - 1, idx)

            def body(b, first, last):
                for pp in range(2):
                    s = b * 2 + pp
                    for j in range(T):
                        for g, part in enumerate(PARTS[j]):
                            if part == "s00" and pp == 0 and j % 2 == 0:
                                dve.wait_ge(S["conv"], n_conv(b, j // 2, True))
                            if part[0] == "s" and (int(part[1]), int(part[2])) in MASKED_BY_DVE:
                                mask(s, j, int(part[1]), int(part[2]))
                            for kind, idx in PLANS[pp][j][g]:
                                if not present(kind, idx, b, pp, first, last):
                                    continue
                                if kind == "fin":
                                    finish(b - 1)
                                else:
                                    item(kind, idx, b, pp)

            dve.wait_ge(S["ident_set"], 1)
            nc.vector.tensor_copy(ident_bf[:], ident[:]).then_inc(S["sel_set"], 1)
            for par in range(2):
                nc.vector.memset(q2[par][DH:P, 0, :].bitcast(F32), 0.0).then_inc(S["sel_set"], 1)
                nc.vector.memset(q2[par][0:DH, 1, :].bitcast(F32), 0.0).then_inc(S["sel_set"], 1)
                nc.vector.tensor_copy(k2[par][DH:P, 0, :], ident[DH:P, DH:DH + 1].to_broadcast([DH, N])).then_inc(S["sel_set"], 1)
                nc.vector.tensor_copy(k2[par][0:DH, 1, :], ident[0:DH, 1:2].to_broadcast([DH, N])).then_inc(S["sel_set"], 1)
            for k in range(4):
                item("prj", k, -1, 0)
            for c in range(3):
                item("v", c, -1, 1)
            for k in range(4):
                item("prj", k, -1, 1)
            for i in range(T):
                for h in range(2):
                    for f in range(2):
                        item("max", (i, h, f), -1, 1)
            for f in range(2):
                item("mt", f, -1, 1)
            drive(nc.vector, body)
            for f in range(2):
                item("l", f, B, 0)
            for c in range(4):
                item("o", c, B, 0)
            finish(B - 1)

        @block.scalar
        def _(act):
            banks = AuxBanks(aux)

            def convert(b, c, transposed):
                g = 4 * transposed + c
                act.wait_ge(adj_in[g % 2], b * 64 + 16 * (g // 2 + 1))
                if not (isinstance(b, int) and b == 0):
                    if transposed:
                        act.wait_ge(S["masked"], n_masked(b * 2 - 1, 2 * c + 1, 1, 1))
                    else:
                        act.wait_ge(S["max_red"], n_max(b * 2 - 1, 2 * c + 1, 1, 1))
                dst = (mask_t if transposed else mask_n)[:, 2 * c:2 * c + 2, :]
                nc.scalar.activation(dst, adj_u8[g % 2][:], ACT.Copy, bias=-BIG, scale=BIG).then_inc(S["conv"], 1)

            def exp(s, pp, j, h, f):
                if h == 0 and f == 0 and not (isinstance(s, int) and s == 0 and j < RING):
                    act.wait_ge(S["pv_done"], s * T + (j - RING + 1))
                    if j < RING:
                        act.wait_ge(S["sum_done"], s * (T - 1) + min(j - RING + T, T - 1) - (T - 1))
                    else:
                        act.wait_ge(S["sum_done"], s * (T - 1) + max(j - RING, 1))
                if (h, f) in MASKED_BY_DVE:
                    act.wait_ge(S["masked"], n_masked(s, j, h, f))
                else:
                    act.wait_ge(S["st_full"], n_unit(s, j, h, f))
                nc.scalar.activation(probs[j % RING][:, h, f * HALF:(f + 1) * HALF], st[h][f][:],
                                     ACT.Exp, scale=SCALE).then_inc(S["p_ready"], 1)

            def item(kind, idx, b, pp):
                s = b * 2 + pp
                bank = banks.next()
                if kind == "mt":
                    act.wait_ge(S["mt_full"], n_half(s + 1, idx))
                    if idx == 0 and isinstance(s, int) and s < 0:
                        act.wait_ge(S["sel_set"], 9)
                    par = (pp + 1) % 2
                    fs = slice(idx * HALF, (idx + 1) * HALF)
                    nc.scalar.mul(q2[par][DH:DH + 2, 0, fs], bank[0:2, :], -1.0).then_inc(S["mrow_done"], 1)
                    nc.scalar.mul(q2[par][0:2, 1, fs], bank[0:2, :], -1.0).then_inc(S["mrow_done"], 1)
                elif kind == "prj":
                    which, f = idx // 2, idx % 2
                    if idx == 0 and not (isinstance(s, int) and s < -1):
                        act.wait_ge(S["op_in"], s * 192 + 384)
                    act.wait_ge(S["prj_full"], n_prj(s + 2, idx))
                    nc.scalar.copy(hi[which][:, f * HALF:(f + 1) * HALF], bank[:]).then_inc(S["hi_done"], 1)
                elif kind == "l":
                    act.wait_ge(S["l_full"], n_half(s - 1, idx))
                    if idx == 0 and not (isinstance(s, int) and s == 1):
                        act.wait_ge(S["n_done"], s - 1)
                    nc.scalar.copy(sums[:, idx * HALF:(idx + 1) * HALF], bank[:]).then_inc(S["l_copied"], 1)
                    if idx == 1:
                        act.wait_ge(S["l_copied"], n_half(s - 1, 1))
                        nc.scalar.activation(rsum[:], sums[:], ACT.Ln).then_inc(S["r_near"], 1)
                        act.wait_ge(S["r_near"], (s - 1) * 2 + 1)
                        nc.scalar.activation(rsum[:], rsum[:], ACT.Exp, scale=-1.0).then_inc(S["r_near"], 1)
                elif kind == "v":
                    bb = b + 1 if pp else b
                    act.wait_ge(S["v_full"], n_four(bb, idx))
                    if not (isinstance(bb, int) and bb == 0):
                        act.wait_ge(S["pv_done"], n_tile(bb * 2 - 1, 2 * idx + 1))
                    nc.scalar.copy(v_sb[:, 2 * idx:2 * idx + 2, :], bank[:].rearrange("p (t d) -> p t d", t=2)).then_inc(S["v_ready"], 1)

            def deviation(b):
                act.wait_ge(S["y_aggr"], b * T + T)
                nc.scalar.activation(std[:], mv[:, :, 1], ACT.Sqrt, bias=eps[:, 0:1], scale=1.0).then_inc(S["std_done"], 1)

            def body(b, first, last):
                for pp in range(2):
                    s = b * 2 + pp
                    for j in range(T):
                        for g, part in enumerate(PARTS[j]):
                            if part[0] == "s":
                                exp(s, pp, j, int(part[1]), int(part[2]))
                            if part == "a1" and j == 0 and not (first and pp == 0):
                                raw_step(b, pp, first)
                            for kind, idx in PLANS[pp][j][g]:
                                if not present(kind, idx, b, pp, first, last):
                                    continue
                                if kind == "fin":
                                    deviation(b - 1)
                                else:
                                    item(kind, idx, b, pp)
                        if not last:
                            if pp == 0 and j >= 4:
                                convert(b + 1, j - 4, False)
                            if pp == 1 and j % 2 == 1:
                                convert(b + 1, j // 2, True)

            def raw_step(b, pp, first):
                s = b * 2 + pp - 1
                q = 1 - pp
                act.wait_ge(S["pv_done"], n_tile(s, T - 1))
                if q == 0 and not first:
                    act.wait_ge(S["o_full"], b * 4)
                for f in range(2):
                    nc.scalar.copy(ot[:, q, f * HALF:(f + 1) * HALF], ot_ps[:, f]).then_inc(S["ot_raw"], 1)

            act.wait_ge(S["const_set"], 3)
            convert(0, 0, False)
            convert(0, 1, False)
            for k in range(4):
                item("prj", k, -1, 0)
            convert(0, 2, False)
            convert(0, 3, False)
            for c in range(3):
                item("v", c, -1, 1)
            for k in range(4):
                item("prj", k, -1, 1)
            for i in range(T * 4):
                banks.next()
            for c in range(4):
                convert(0, c, True)
            for f in range(2):
                item("mt", f, -1, 1)
            drive(nc.scalar, body)
            raw_step(B, 0, False)
            for f in range(2):
                item("l", f, B, 0)
            deviation(B - 1)

        @block.gpsimd
        def _(pool):
            nc.gpsimd.memset(ones[:], 1.0).then_inc(S["const_set"], 1)
            nc.gpsimd.memset(eps[:], EPS).then_inc(S["const_set"], 1)
            nc.gpsimd.memset(two[:], 2.0).then_inc(S["const_set"], 1)
            nc.gpsimd.memset(ident0[:], 1.0).then_inc(S["w_pool"], 1)
            pool.wait_ge(S["w_pool"], 1)
            nc.gpsimd.affine_select(out=ident[:], in_=ident0[:], compare_op=ALU.is_equal, fill=0.0, base=0,
                                    pattern=[[-1, P]], channel_multiplier=1).then_inc(S["ident_set"], 1)
            pool.wait_ge(S["bias_in"], 16)

            def normalise(s, pp):
                def link(n):
                    pool.wait_ge(S["newton"], s * 3 + n)

                pool.wait_ge(S["r_near"], s * 2 + 2)
                nc.gpsimd.tensor_tensor(out=sums[:], in0=sums[:], in1=rsum[:], op=ALU.mult).then_inc(S["newton"], 1)
                link(1)
                nc.gpsimd.tensor_tensor(out=sums[:], in0=two[:, 0:1].to_broadcast([P, N]), in1=sums[:], op=ALU.subtract).then_inc(S["newton"], 1)
                link(2)
                nc.gpsimd.tensor_tensor(out=rsum[:], in0=rsum[:], in1=sums[:], op=ALU.mult).then_inc(S["newton"], 1)
                link(3)
                pool.wait_ge(S["ot_raw"], n_half(s, 1))
                nc.gpsimd.tensor_tensor(out=ot[:, pp, :], in0=ot[:, pp, :], in1=rsum[:], op=ALU.mult).then_inc(S["n_done"], 1)

            def body(b, first, last):
                for pp in range(2):
                    s = b * 2 + pp
                    for j in range(1, T):
                        pool.wait_ge(S["p_ready"], n_unit(s, j, 1, 1))
                        if j == 1:
                            if not (first and pp == 0):
                                pool.wait_ge(S["l_full"], n_half(s - 1, 1))
                        else:
                            pool.wait_ge(S["sum_done"], s * (T - 1) + (j - 1))
                        in0 = probs[0] if j == 1 else psums
                        nc.gpsimd.tensor_tensor(out=psums[:], in0=in0[:], in1=probs[j % RING][:], op=ALU.add).then_inc(S["sum_done"], 1)
                        if j == 3 and not (first and pp == 0):
                            normalise(s - 1, 1 - pp)
                    if pp == 1:
                        pool.wait_ge(S["x_in"], b * 16 + 16)
                        nc.gpsimd.tensor_tensor(out=y[:], in0=y[:], in1=bias_row[:].rearrange("p (a d) -> p a d", a=1).to_broadcast([P, T, D]),
                                                op=ALU.add).then_inc(S["xb_done"], 1)

            drive(nc.gpsimd, body)
            normalise(2 * B - 1, 1)


_OUT = ((8, 1024, 256), "float32")


def kernel(x, adj, L0_gnn_Wq, L0_gnn_Wk, L0_gnn_Wv, L0_gnn_Wo, L0_gnn_bo):
    import numpy as _np
    import concourse.bacc as _bacc
    from concourse import mybir as _mybir
    from concourse.bass_utils import run_bass_kernel_spmd as _run

    nc = _bacc.Bacc("TRN2", target_bir_lowering=False, num_devices=1)
    x, adj = _np.asarray(x), _np.asarray(adj)
    sent = {
        "xt": x.transpose(0, 2, 1), "x": x, "adj": adj, "adjt": adj.transpose(0, 2, 1),
        "wq": L0_gnn_Wq, "wk": L0_gnn_Wk, "wv": L0_gnn_Wv, "wo": L0_gnn_Wo, "bo": L0_gnn_bo,
    }
    arrays, args = {}, []
    for name, a in sent.items():
        a = _np.ascontiguousarray(a)
        arrays[f"in_{name}_dram"] = a
        args.append(nc.dram_tensor(f"in_{name}_dram", a.shape, _mybir.dt.from_np(a.dtype), kind="ExternalInput").ap())
    args.append(nc.dram_tensor("out_0_dram", _OUT[0], _mybir.dt.from_np(_np.dtype(_OUT[1])), kind="ExternalOutput").ap())
    masked_attention_residual_norm(nc, *args)
    r = _run(nc, [arrays], core_ids=[0])
    return r.results[0]["out_0_dram"]
```

```python
from contextlib import ExitStack

import concourse.bass as bass
from concourse import mybir

F32 = mybir.dt.float32
F32R = mybir.dt.float32r
BF16 = mybir.dt.bfloat16
U8 = mybir.dt.uint8
ALU = mybir.AluOpType
ACT = mybir.ActivationFunctionType
AX_X = mybir.AxisListType.X

P = 128
HALF = 512
BIG = 2.0 ** 100
EPS = 1e-5


def slot_plan(pp):
    plan = [[[] for _ in range(6)] for _ in range(8)]
    maxima = [("max", (i, h, f)) for i in range(8) for h in range(2) for f in range(2)]
    for s, places in MAXIMA:
        for at in places:
            plan[s][at].append(maxima.pop(0))
    assert not maxima
    for kind, idx, s, at in MORE[pp]:
        plan[s][at].append((kind, idx))
    return plan


MAXIMA = [(1, (2, 3, 4, 5))] + [(s, (1, 2, 3, 4, 5)) for s in range(2, 7)] + [(7, (1, 2, 3))]
MORE = [
    [("v", 3, 1, 0), ("l", 0, 2, 5), ("l", 1, 3, 0), ("prj", 0, 4, 0), ("prj", 1, 5, 0), ("prj", 2, 6, 0),
     ("prj", 3, 7, 0), ("mt", 0, 7, 5), ("mt", 1, 7, 5), ("o", 0, 6, 5), ("o", 1, 7, 2)],
    [("o", 2, 0, 0), ("o", 3, 0, 0), ("fin", 0, 1, 0), ("l", 0, 2, 5), ("l", 1, 3, 0), ("v", 0, 3, 2), ("prj", 0, 4, 0),
     ("prj", 1, 5, 0), ("prj", 2, 6, 0), ("prj", 3, 7, 0), ("mt", 0, 7, 5), ("mt", 1, 7, 5), ("v", 1, 5, 2), ("v", 2, 7, 2)],
]
LAST_SUMS = {3: (1,), 4: (2, 3), 5: (4,), 6: (5,), 7: (6,)}
PROLOGUE_MORE = {0: [("conv", 3, False)], 1: [("prj", 0, 1)], 2: [("prj", 1, 1)], 3: [("prj", 2, 1)],
                 4: [("prj", 3, 1), ("conv", 0, True)], 5: [("conv", 1, True)], 6: [("conv", 2, True)]}
PARTS = [["a0", "s00", "s01", "a1", "s10", "s11"]] + [["s00", "s01", "a0", "s10", "s11", "a1"]] * 7
PLANS = [slot_plan(0), slot_plan(1)]
MASKED_BY_PE = [(0, 1), (1, 0)]
MASKED_BY_DVE = [(h, f) for h in range(2) for f in range(2) if (h, f) not in MASKED_BY_PE]


class AuxBanks:

    def __init__(self, banks):
        self.banks, self.n, self.held_by = banks, 0, [None] * len(banks)

    def next(self):
        self.n += 1
        return self.banks[(self.n - 1) % len(self.banks)]

    def take(self, item):
        k = self.n % len(self.banks)
        before, self.held_by[k] = self.held_by[k], item
        return self.next(), before

    def enter_loop(self, b):
        self.held_by = [(kind, idx, b - 1, pp) for kind, idx, _, pp in self.held_by]


def masked_attention_residual_norm(nc, xt, x, adj, adjt, wq, wk, wv, wo, bo, out):
    B, N, D = x.shape
    H = 4
    DH = D // H
    PAIRS = H // 2
    T = N // P
    KT = D // P
    SCALE = DH ** -0.5
    RING = 4
    assert T == 8 and KT == 2 and DH == 64 and PAIRS == 2 and N == 2 * HALF

    xt_v = xt.rearrange("b (k p) n -> b p k n", p=P)
    x_v = x.rearrange("b (t p) d -> b p t d", p=P)
    out_v = out.rearrange("b (t p) d -> b p t d", p=P)
    adj_v = adj.rearrange("b (c t p) n -> b c p t n", p=P, t=2)
    adjt_v = adjt.rearrange("b (c t p) n -> b c p t n", p=P, t=2)
    w_v = [w.rearrange("(k p) n -> p k n", p=P) for w in (wq, wk, wv, wo)]

    with ExitStack() as ctx:
        def sb(name, shape, dt=F32):
            return ctx.enter_context(nc.sbuf_tensor(name, shape, dt))

        def psum(name, shape):
            return ctx.enter_context(nc.psum_tensor(name, shape, F32))

        def sem(name):
            return ctx.enter_context(nc.semaphore(name))

        w_sb = [sb(f"w{n}", [P, KT, D]) for n in ("q", "k", "v", "o")]
        bias_row = sb("bias_row", [P, D])
        ident = sb("ident", [P, P])
        ident0 = sb("ident0", [P, P])
        ident_bf = sb("ident_bf", [P, P], BF16)
        ones = sb("ones", [P, DH])
        eps = sb("eps", [P, 1])
        two = sb("two", [P, 1])
        xt_sb = sb("xt_sb", [P, KT, N])
        adj_u8 = [sb(f"adj_u8_{i}", [P, 2, N], U8) for i in range(2)]
        mask_n = sb("mask_n", [P, T, N], BF16)
        mask_t = sb("mask_t", [P, T, N], BF16)
        qk1 = [sb(f"qk1_{i}", [P, 2, 2, N], F32R) for i in range(2)]
        qk2 = [sb(f"qk2_{i}", [P, 2, 2, N], F32R) for i in range(2)]
        q1 = [t[:, 0] for t in qk1]
        k1 = [t[:, 1] for t in qk1]
        q2 = [t[:, 0] for t in qk2]
        k2 = [t[:, 1] for t in qk2]
        staged = sb("staged", [P, 4, N], F32R)
        hi = [staged[:, 0], staged[:, 2]]
        lo = [staged[:, 1], staged[:, 3]]
        v_sb = sb("v_sb", [P, T, D])
        probs = [sb(f"probs{i}", [P, 2, N]) for i in range(RING)]
        psums = sb("psums", [P, 2, N])
        ot = sb("ot", [P, PAIRS, N])
        sums = sb("sums", [P, N])
        rsum = sb("rsum", [P, N])
        y = sb("y", [P, T, D])
        mx = sb("mx", [P, T, 2, 2])
        m = sb("m", [P, T, 2])
        stats = sb("stats", [P, T, 6])
        mv = sb("mv", [P, T, 2])
        std = sb("std", [P, T])
        rstd = sb("rstd", [P, T])

        st = [[psum(f"st{h}{f}", [P, HALF]) for f in range(2)] for h in range(2)]
        ot_ps = psum("ot_ps", [P, 2, HALF])
        aux = [psum(f"aux{i}", [P, HALF]) for i in range(2)]

        all_banks = aux + st[0] + st[1]

        names = ("wq_in wk_in wv_in wo_in bias_in xt_in adj_in0 adj_in1 x_in out_st op_in w_pool apart ident_set const_set sel_set "
                 "st_full pv_done max_full mt_full prj_full v_full l_full o_full "
                 "masked max_red m_done lo_done r_done n_done half_done l_copied r_near newton y_sum y_stat y_aggr y_rstd y_done "
                 "p_ready hi_done mrow_done v_ready ot_raw conv std_done sum_done xb_done")
        S = {n: sem(n) for n in names.split()}
        w_in = [S["wq_in"], S["wk_in"], S["wv_in"], S["wo_in"]]
        adj_in = [S["adj_in0"], S["adj_in1"]]

        def n_unit(s, j, h, f):
            return s * 32 + (4 * j + 2 * h + f + 1)

        def n_masked(s, j, h, f):
            per_tile = len(MASKED_BY_DVE)
            return s * (T * per_tile) + (j * per_tile + MASKED_BY_DVE.index((h, f)) + 1)

        def n_tile(s, j):
            return s * T + (j + 1)

        def n_max(s, i, h, f):
            return s * 32 + (4 * i + 2 * h + f + 1)

        def n_half(s, f):
            return s * 2 + (f + 1)

        def n_row(s, f):
            return s * 4 + (2 * f + 2)

        def n_prj(s, k):
            return s * 4 + (k + 1)

        def n_four(b, c):
            return b * 4 + (c + 1)

        def n_conv(b, c, transposed):
            return b * 8 + (4 * transposed + c + 1)

        def reader_of(kind, idx, b, pp):
            s = b * 2 + pp
            if kind == "max":
                return S["max_red"], n_max(s + 1, *idx)
            if kind == "mt":
                return S["mrow_done"], n_row(s + 1, idx)
            if kind == "prj":
                return S["lo_done"], n_prj(s + 2, idx)
            if kind == "v":
                return S["v_ready"], n_four(b + 1 if pp else b, idx)
            if kind == "l":
                return S["l_copied"], n_half(s - 1, idx)
            return S["y_sum"], n_four(b - 1, idx)

        def present(kind, idx, b, pp, first, last):
            if kind in ("max", "mt"):
                return not (last and pp == 1)
            if kind == "prj":
                return not last
            if kind == "v":
                return not (last and pp == 1)
            if kind == "l":
                return not (first and pp == 0)
            return not first

        def drive(engine, body, banks=None):
            body(0, True, False)
            with engine.Fori(1, B - 1) as b:
                if banks is not None:
                    banks.enter_loop(b)
                body(b, False, False)
            if banks is not None:
                banks.enter_loop(B - 1)
            body(B - 1, False, True)

        def wait_apart(engine, semaphore, value):
            engine.wait_ge(semaphore, value)
            if not isinstance(value, int):
                engine.sem_inc(S["apart"], 1)

        prologue = [("conv", 0, False)] + [("prj", k, 0) for k in range(4)] + [("conv", 1, False)]
        prologue += [("v", c, 1) for c in range(3)] + [("conv", 2, False)]
        for i in range(T):
            prologue += [("max", (i, h, f), 1) for h in range(2) for f in range(2)]
            prologue += PROLOGUE_MORE.get(i, [])
        prologue += [("mt", f, 1) for f in range(2)]

        block = ctx.enter_context(nc.Block())

        @block.sync
        def _(sp):
            def load_adj(b, c, transposed):
                g = 4 * transposed + c
                if not (isinstance(b, int) and b == 0 and g < 2):
                    wait_apart(sp, S["conv"], b * 8 + (g - 1))
                src = (adjt_v if transposed else adj_v)[b, c]
                sp.dma_start(adj_u8[g % 2][:], src).then_inc(adj_in[g % 2], 16)

            def load_ops(s, par):
                sp.wait_ge(S["hi_done"], n_prj(s, 3))
                sp.wait_ge(S["lo_done"], n_prj(s, 3))
                if not isinstance(s, int) or s >= 2:
                    sp.wait_ge(S["st_full"], n_unit(s - 2, T - 1, 1, 1))
                for h in range(2):
                    own, other = (slice(h * DH, (h + 1) * DH), slice((1 - h) * DH, (2 - h) * DH))
                    for src, dst in (
                        (staged[own, 0::2], qk1[par][own, :, h]),
                        (staged[own, 1:3], qk1[par][other, :, h]),
                        (staged[own, 0::3], qk2[par][own, :, h]),
                    ):
                        sp.dma_start(dst.bitcast(F32), src.bitcast(F32)).then_inc(S["op_in"], 16)

            def store(b):
                for f in range(2):
                    wait_apart(sp, S["y_done"], b * T + (T // 2) * (f + 1))
                    h = slice(f * T // 2, (f + 1) * T // 2)
                    sp.dma_start(out_v[b][:, h], y[:, h]).then_inc(S["out_st"], 16)

            def body(b, first, last):
                if not last:
                    wait_apart(sp, S["v_full"], n_four(b, 3))
                    sp.dma_start(xt_sb[:], xt_v[b + 1]).then_inc(S["xt_in"], 16)
                    for c in range(4):
                        load_adj(b + 1, c, False)
                load_ops_next = not last
                if load_ops_next:
                    load_ops(b * 2 + 2, 0)
                if not first:
                    store(b - 1)
                    wait_apart(sp, S["out_st"], b * 32)
                sp.dma_start(y[:], x_v[b]).then_inc(S["x_in"], 16)
                if not last:
                    for c in range(4):
                        load_adj(b + 1, c, True)
                    load_ops(b * 2 + 3, 1)

            sp.dma_start(xt_sb[:], xt_v[0]).then_inc(S["xt_in"], 16)
            for n in range(4):
                sp.dma_start(w_sb[n][:], w_v[n]).then_inc(w_in[n], 16)
            sp.dma_start(bias_row[:], bo.rearrange("(a d) -> a d", a=1).to_broadcast([P, D])).then_inc(S["bias_in"], 16)
            for c in range(4):
                load_adj(0, c, False)
            load_ops(0, 0)
            for c in range(4):
                load_adj(0, c, True)
            load_ops(1, 1)
            drive(nc.sync, body)
            store(B - 1)
            sp.wait_ge(S["out_st"], B * 32)

        @block.tensor
        def _(pe):
            banks = AuxBanks(all_banks)

            def scores(s, pp, j, h, f):
                if h == 0 and f == 0 and j == 0:
                    pe.wait_ge(S["mrow_done"], n_row(s, 1))
                if not (isinstance(s, int) and s == 0 and j == 0):
                    pe.wait_ge(S["p_ready"], n_unit(s, j, h, f) - 4)
                js, fs = slice(j * P, (j + 1) * P), slice(f * HALF, (f + 1) * HALF)
                by_dve = (h, f) in MASKED_BY_DVE
                nc.tensor.matmul(st[h][f][:], k1[pp][:, h, js], q1[pp][:, h, fs], start=True, stop=False)
                done = nc.tensor.matmul(st[h][f][:], k2[pp][:, h, js], q2[pp][:, h, fs], start=False, stop=by_dve)
                if not by_dve:
                    done = nc.tensor.matmul(st[h][f][:], ident_bf[:], mask_t[:, j, fs], start=False, stop=True)
                done.then_inc(S["st_full"], 1)

            def attend(s, pp, j, f):
                pe.wait_ge(S["p_ready"], n_unit(s, j, 1, f))
                if f == 0:
                    if j % 2 == 0 and pp == 0:
                        pe.wait_ge(S["v_ready"], s * 2 + (j // 2 + 1))
                    if j == 0 and not (isinstance(s, int) and s == 0):
                        pe.wait_ge(S["ot_raw"], n_half(s - 1, 1))
                fs = slice(f * HALF, (f + 1) * HALF)
                for h in range(2):
                    c = (pp * 2 + h) * DH
                    last = nc.tensor.matmul(ot_ps[h * DH:(h + 1) * DH, f], v_sb[:, j, c:c + DH],
                                            probs[j % RING][:, h, fs], start=(j == 0), stop=(j == T - 1))
                if f == 1:
                    last.then_inc(S["pv_done"], 1)

            def item(kind, idx, b, pp):
                s = b * 2 + pp
                bank, before = banks.take((kind, idx, b, pp))
                if before is not None:
                    pe.wait_ge(*reader_of(*before))
                if kind == "max":
                    i, h, f = idx
                    par = (pp + 1) % 2
                    if i == 0 and h == 0 and f == 0:
                        pe.wait_ge(S["op_in"], s * 96 + 192)
                    nc.tensor.matmul(bank[:], q1[par][:, h, i * P:(i + 1) * P], k1[par][:, h, f * HALF:(f + 1) * HALF],
                                     start=True, stop=True).then_inc(S["max_full"], 1)
                elif kind == "mt":
                    if idx == 0:
                        if isinstance(s, int) and s < 0:
                            pe.wait_ge(S["ident_set"], 1)
                        pe.wait_ge(S["m_done"], s + 2)
                    for t in range(4):
                        last = nc.tensor.transpose(bank[0:2, t * P:(t + 1) * P], m[:, 4 * idx + t, :], ident[:])
                    last.then_inc(S["mt_full"], 1)
                elif kind == "prj":
                    which, f = idx // 2, idx % 2
                    par = pp
                    if idx == 0 and par == 0:
                        pe.wait_ge(S["xt_in"], b * 16 + 32)
                    for k in range(KT):
                        last = nc.tensor.matmul(bank[:], w_sb[which][:, k, par * P:(par + 1) * P],
                                                xt_sb[:, k, f * HALF:(f + 1) * HALF], start=(k == 0), stop=(k == KT - 1))
                    last.then_inc(S["prj_full"], 1)
                elif kind == "v":
                    for t in range(2):
                        j = 2 * idx + t
                        for k in range(KT):
                            last = nc.tensor.matmul(bank[:, t * D:(t + 1) * D], xt_sb[:, k, j * P:(j + 1) * P],
                                                    w_sb[2][:, k, :], start=(k == 0), stop=(k == KT - 1))
                    last.then_inc(S["v_full"], 1)
                elif kind == "l":
                    if idx == 0:
                        pe.wait_ge(S["sum_done"], (s - 1) * (T - 1) + (T - 1))
                    for h in range(2):
                        last = nc.tensor.matmul(bank[h * DH:(h + 1) * DH, :], ones[:], psums[:, h, idx * HALF:(idx + 1) * HALF],
                                                start=True, stop=True)
                    last.then_inc(S["l_full"], 1)
                else:
                    if isinstance(b, int) and b == B:
                        pe.wait_ge(S["n_done"], 2 * B - 1)
                        pe.wait_ge(S["half_done"], idx // 2 + 1)
                    elif idx == 0:
                        pe.wait_ge(S["n_done"], b * 2)
                    for t in range(2):
                        i = 2 * idx + t
                        for k in range(KT):
                            last = nc.tensor.matmul(bank[:, t * D:(t + 1) * D], ot[:, k, i * P:(i + 1) * P],
                                                    w_sb[3][:, k, :], start=(k == 0), stop=(k == KT - 1))
                    last.then_inc(S["o_full"], 1)

            def body(b, first, last):
                for pp in range(2):
                    s = b * 2 + pp
                    for j in range(T):
                        for g, part in enumerate(PARTS[j]):
                            if part == "s00" and pp == 0 and j % 2 == 0:
                                pe.wait_ge(S["conv"], n_conv(b, j // 2, True))
                            if part[0] == "s":
                                scores(s, pp, j, int(part[1]), int(part[2]))
                            elif j > 0:
                                attend(s, pp, j - 1, int(part[1]))
                            elif not (first and pp == 0):
                                attend(s - 1, 1 - pp, T - 1, int(part[1]))
                            for kind, idx in PLANS[pp][j][g]:
                                if kind != "fin" and present(kind, idx, b, pp, first, last):
                                    item(kind, idx, b, pp)

            pe.wait_ge(S["wq_in"], 16)
            pe.wait_ge(S["xt_in"], 16)
            for kind, idx, pp in prologue:
                if kind == "conv":
                    continue
                if pp == 0 and idx == 2:
                    pe.wait_ge(S["wk_in"], 16)
                if kind == "v" and idx == 0:
                    pe.wait_ge(S["wv_in"], 16)
                item(kind, idx, -1, pp)
            pe.wait_ge(S["max_red"], n_max(0, T - 1, 1, 1))
            pe.wait_ge(S["mrow_done"], n_row(0, 1))
            pe.wait_ge(S["wo_in"], 16)
            pe.wait_ge(S["const_set"], 3)
            banks = AuxBanks(aux)
            pe.wait_ge(S["sel_set"], 9)
            drive(nc.tensor, body, banks)
            attend(2 * B - 1, 1, T - 1, 0)
            attend(2 * B - 1, 1, T - 1, 1)
            for f in range(2):
                item("l", f, B, 0)
            for c in range(4):
                item("o", c, B, 0)

        @block.vector
        def _(dve):
            banks = AuxBanks(all_banks)

            def mask(s, j, h, f):
                dve.wait_ge(S["st_full"], n_unit(s, j, h, f))
                nc.vector.tensor_tensor(out=st[h][f][:], in0=st[h][f][:], in1=mask_t[:, j, f * HALF:(f + 1) * HALF],
                                        op=ALU.add).then_inc(S["masked"], 1)

            def sum_tile(j):
                dve.wait_ge(S["p_ready"], n_unit(2 * B - 1, j, 1, 1))
                if j == 1:
                    dve.wait_ge(S["l_full"], n_half(2 * B - 2, 1))
                else:
                    dve.wait_ge(S["sum_done"], (2 * B - 1) * (T - 1) + (j - 1))
                nc.vector.tensor_tensor(out=psums[:], in0=(probs[0] if j == 1 else psums)[:], in1=probs[j % RING][:],
                                        op=ALU.add).then_inc(S["sum_done"], 1)

            def norm(b, c):
                for t in range(2 * c, 2 * c + 2):
                    nc.vector.bn_stats(stats[:, t, :], y[:, t, :]).then_inc(S["y_stat"], 1)

            def aggregate(b, tiles):
                wait_apart(dve, S["y_stat"], b * T + tiles.stop)
                for t in range(T)[tiles]:
                    nc.vector.bn_aggr(mv[:, t, :], stats[:, t, :]).then_inc(S["y_aggr"], 1)

            def finish(tiles, count):
                dve.wait_ge(S["std_done"], count)
                nc.vector.reciprocal(rstd[:, tiles], std[:, tiles]).then_inc(S["y_rstd"], 1)
                dve.wait_ge(S["y_rstd"], count)
                for t in range(T)[tiles]:
                    nc.vector.tensor_scalar(y[:, t, :], y[:, t, :], mv[:, t, 0:1], rstd[:, t:t + 1],
                                            ALU.subtract, ALU.mult).then_inc(S["y_done"], 1)

            def item(kind, idx, b, pp):
                s = b * 2 + pp
                bank = banks.next()
                if kind == "max":
                    i, h, f = idx
                    if h == 0 and f == 0 and i % 2 == 0:
                        dve.wait_ge(S["conv"], n_conv(b + pp, i // 2, False))
                    if i == 0 and h == 0 and f == 0 and not (isinstance(s, int) and s < 0):
                        dve.wait_ge(S["m_done"], s + 1)
                    wait_apart(dve, S["max_full"], n_max(s + 1, i, h, f))
                    nc.vector.tensor_tensor_reduce(
                        out=bank[:], in0=bank[:], in1=mask_n[:, i, f * HALF:(f + 1) * HALF], scale=1.0,
                        scalar=-3.0e38, op0=ALU.add, op1=ALU.max, accum_out=mx[:, i, h, f:f + 1]).then_inc(S["max_red"], 1)
                    if i == T - 1 and h == 1 and f == 1:
                        dve.wait_ge(S["max_red"], n_max(s + 1, i, h, f))
                        if not (isinstance(s, int) and s < 0):
                            dve.wait_ge(S["mt_full"], n_half(s, 1))
                        nc.vector.tensor_reduce(m[:], mx[:], AX_X, ALU.max).then_inc(S["m_done"], 1)
                elif kind == "prj":
                    which, f = idx // 2, idx % 2
                    fs = slice(f * HALF, (f + 1) * HALF)
                    if idx == 0 and not (isinstance(s, int) and s < -1):
                        dve.wait_ge(S["op_in"], s * 96 + 192)
                    dve.wait_ge(S["hi_done"], n_prj(s + 2, idx))
                    nc.vector.tensor_tensor(out=lo[which][:, fs], in0=bank[:], in1=hi[which][:, fs].bitcast(F32),
                                            op=ALU.subtract).then_inc(S["lo_done"], 1)
                elif kind == "o":
                    if idx == 0:
                        dve.wait_ge(S["xb_done"], b)
                    dve.wait_ge(S["o_full"], n_four(b - 1, idx))
                    ys = y[:, 2 * idx:2 * idx + 2, :]
                    nc.vector.tensor_tensor(out=ys, in0=bank[:].rearrange("p (t d) -> p t d", t=2), in1=ys,
                                            op=ALU.add).then_inc(S["y_sum"], 1)
                    dve.wait_ge(S["y_sum"], n_four(b - 1, idx))
                    norm(b - 1, idx)

            def body(b, first, last):
                for pp in range(2):
                    s = b * 2 + pp
                    for j in range(T):
                        for g, part in enumerate(PARTS[j]):
                            if part == "s00" and pp == 0 and j % 2 == 0:
                                dve.wait_ge(S["conv"], n_conv(b, j // 2, True))
                            if part[0] == "s" and (int(part[1]), int(part[2])) in MASKED_BY_DVE:
                                mask(s, j, int(part[1]), int(part[2]))
                            if part == "s11" and last and pp == 1:
                                for tile in LAST_SUMS.get(j, ()):
                                    sum_tile(tile)
                            for kind, idx in PLANS[pp][j][g]:
                                if not present(kind, idx, b, pp, first, last):
                                    continue
                                if kind == "fin":
                                    aggregate(b - 1, slice(0, T))
                                    finish(slice(0, T), b)
                                else:
                                    item(kind, idx, b, pp)

            dve.wait_ge(S["ident_set"], 1)
            nc.vector.tensor_copy(ident_bf[:], ident[:]).then_inc(S["sel_set"], 1)
            for par in range(2):
                nc.vector.memset(q2[par][DH:P, 0, :].bitcast(F32), 0.0).then_inc(S["sel_set"], 1)
                nc.vector.memset(q2[par][0:DH, 1, :].bitcast(F32), 0.0).then_inc(S["sel_set"], 1)
                nc.vector.tensor_copy(k2[par][DH:P, 0, :], ident[DH:P, DH:DH + 1].to_broadcast([DH, N])).then_inc(S["sel_set"], 1)
                nc.vector.tensor_copy(k2[par][0:DH, 1, :], ident[0:DH, 1:2].to_broadcast([DH, N])).then_inc(S["sel_set"], 1)
            for kind, idx, pp in prologue:
                if kind != "conv":
                    item(kind, idx, -1, pp)
            banks = AuxBanks(aux)
            drive(nc.vector, body)
            sum_tile(T - 1)
            for f in range(2):
                bank, fs = banks.next(), slice(f * HALF, (f + 1) * HALF)
                dve.wait_ge(S["l_full"], n_half(2 * B - 1, f))
                if f == 0:
                    dve.wait_ge(S["n_done"], 2 * B - 1)
                nc.vector.reciprocal(rsum[:, fs], bank[:]).then_inc(S["l_copied"], 1)
                dve.wait_ge(S["l_copied"], n_half(2 * B - 1, f))
                dve.wait_ge(S["ot_raw"], n_half(2 * B - 1, f))
                nc.vector.tensor_tensor(out=ot[:, 1, fs], in0=ot[:, 1, fs], in1=rsum[:, fs], op=ALU.mult).then_inc(S["half_done"], 1)
            early, late = slice(0, T // 2), slice(T // 2, T)
            item("o", 0, B, 0)
            item("o", 1, B, 0)
            aggregate(B - 1, early)
            item("o", 2, B, 0)
            finish(early, B)
            item("o", 3, B, 0)
            aggregate(B - 1, late)
            finish(late, B + 1)

        @block.scalar
        def _(act):
            banks = AuxBanks(all_banks)

            def convert(b, c, transposed):
                g = 4 * transposed + c
                act.wait_ge(adj_in[g % 2], b * 64 + 16 * (g // 2 + 1))
                if not (isinstance(b, int) and b == 0):
                    if transposed:
                        act.wait_ge(S["st_full"], n_unit(b * 2 - 1, 2 * c + 1, 1, 1))
                        act.wait_ge(S["masked"], n_masked(b * 2 - 1, 2 * c + 1, *MASKED_BY_DVE[-1]))
                    else:
                        act.wait_ge(S["max_red"], n_max(b * 2 - 1, 2 * c + 1, 1, 1))
                dst = (mask_t if transposed else mask_n)[:, 2 * c:2 * c + 2, :]
                nc.scalar.activation(dst, adj_u8[g % 2][:], ACT.Copy, bias=-BIG, scale=BIG).then_inc(S["conv"], 1)

            def exp(s, pp, j, h, f):
                if h == 0 and f == 0 and not (isinstance(s, int) and s == 0 and j < RING):
                    act.wait_ge(S["pv_done"], s * T + (j - RING + 1))
                    if j < RING:
                        act.wait_ge(S["sum_done"], s * (T - 1) + min(j - RING + T, T - 1) - (T - 1))
                    else:
                        act.wait_ge(S["sum_done"], s * (T - 1) + max(j - RING, 1))
                if (h, f) in MASKED_BY_DVE:
                    act.wait_ge(S["masked"], n_masked(s, j, h, f))
                else:
                    act.wait_ge(S["st_full"], n_unit(s, j, h, f))
                nc.scalar.activation(probs[j % RING][:, h, f * HALF:(f + 1) * HALF], st[h][f][:],
                                     ACT.Exp, scale=SCALE).then_inc(S["p_ready"], 1)

            def item(kind, idx, b, pp):
                s = b * 2 + pp
                bank = banks.next()
                if kind == "mt":
                    act.wait_ge(S["mt_full"], n_half(s + 1, idx))
                    if idx == 0 and isinstance(s, int) and s < 0:
                        act.wait_ge(S["sel_set"], 9)
                    par = (pp + 1) % 2
                    fs = slice(idx * HALF, (idx + 1) * HALF)
                    nc.scalar.mul(q2[par][DH:DH + 2, 0, fs], bank[0:2, :], -1.0).then_inc(S["mrow_done"], 1)
                    nc.scalar.mul(q2[par][0:2, 1, fs], bank[0:2, :], -1.0).then_inc(S["mrow_done"], 1)
                elif kind == "prj":
                    which, f = idx // 2, idx % 2
                    if idx == 0 and not (isinstance(s, int) and s < -1):
                        act.wait_ge(S["op_in"], s * 96 + 192)
                    act.wait_ge(S["prj_full"], n_prj(s + 2, idx))
                    nc.scalar.copy(hi[which][:, f * HALF:(f + 1) * HALF], bank[:]).then_inc(S["hi_done"], 1)
                elif kind == "l":
                    act.wait_ge(S["l_full"], n_half(s - 1, idx))
                    if idx == 0 and not (isinstance(s, int) and s == 1):
                        act.wait_ge(S["n_done"], s - 1)
                    nc.scalar.copy(sums[:, idx * HALF:(idx + 1) * HALF], bank[:]).then_inc(S["l_copied"], 1)
                    if idx == 1:
                        act.wait_ge(S["l_copied"], n_half(s - 1, 1))
                        nc.scalar.activation(rsum[:], sums[:], ACT.Ln).then_inc(S["r_near"], 1)
                        act.wait_ge(S["r_near"], (s - 1) * 2 + 1)
                        nc.scalar.activation(rsum[:], rsum[:], ACT.Exp, scale=-1.0).then_inc(S["r_near"], 1)
                elif kind == "v":
                    bb = b + 1 if pp else b
                    act.wait_ge(S["v_full"], n_four(bb, idx))
                    if not (isinstance(bb, int) and bb == 0):
                        act.wait_ge(S["pv_done"], n_tile(bb * 2 - 1, 2 * idx + 1))
                    nc.scalar.copy(v_sb[:, 2 * idx:2 * idx + 2, :], bank[:].rearrange("p (t d) -> p t d", t=2)).then_inc(S["v_ready"], 1)

            def deviation(b, tiles):
                act.wait_ge(S["y_aggr"], b * T + tiles.stop)
                nc.scalar.activation(std[:, tiles], mv[:, tiles, 1], ACT.Sqrt, bias=eps[:, 0:1], scale=1.0).then_inc(S["std_done"], 1)

            def body(b, first, last):
                for pp in range(2):
                    s = b * 2 + pp
                    for j in range(T):
                        for g, part in enumerate(PARTS[j]):
                            if part[0] == "s":
                                exp(s, pp, j, int(part[1]), int(part[2]))
                            if part == "a1" and j == 0 and not (first and pp == 0):
                                raw_step(b, pp, first)
                            for kind, idx in PLANS[pp][j][g]:
                                if not present(kind, idx, b, pp, first, last):
                                    continue
                                if kind == "fin":
                                    deviation(b - 1, slice(0, T))
                                else:
                                    item(kind, idx, b, pp)
                        if not last:
                            if pp == 0 and j >= 4:
                                convert(b + 1, j - 4, False)
                            if pp == 1 and j % 2 == 1:
                                convert(b + 1, j // 2, True)

            def raw_step(b, pp, first):
                s = b * 2 + pp - 1
                q = 1 - pp
                act.wait_ge(S["pv_done"], n_tile(s, T - 1))
                if q == 0 and not first:
                    act.wait_ge(S["o_full"], b * 4)
                for f in range(2):
                    nc.scalar.copy(ot[:, q, f * HALF:(f + 1) * HALF], ot_ps[:, f]).then_inc(S["ot_raw"], 1)

            act.wait_ge(S["const_set"], 3)
            for kind, idx, pp in prologue:
                if kind == "conv":
                    convert(0, idx, pp)
                else:
                    item(kind, idx, -1, pp)
            convert(0, 3, True)
            banks = AuxBanks(aux)
            drive(nc.scalar, body)
            raw_step(B, 0, False)
            deviation(B - 1, slice(0, T // 2))
            deviation(B - 1, slice(T // 2, T))

        @block.gpsimd
        def _(pool):
            nc.gpsimd.memset(ones[:], 1.0).then_inc(S["const_set"], 1)
            nc.gpsimd.memset(eps[:], EPS).then_inc(S["const_set"], 1)
            nc.gpsimd.memset(two[:], 2.0).then_inc(S["const_set"], 1)
            nc.gpsimd.memset(ident0[:], 1.0).then_inc(S["w_pool"], 1)
            pool.wait_ge(S["w_pool"], 1)
            nc.gpsimd.affine_select(out=ident[:], in_=ident0[:], compare_op=ALU.is_equal, fill=0.0, base=0,
                                    pattern=[[-1, P]], channel_multiplier=1).then_inc(S["ident_set"], 1)
            pool.wait_ge(S["bias_in"], 16)

            def normalise(s, pp):
                def link(n):
                    pool.wait_ge(S["newton"], s * 3 + n)

                pool.wait_ge(S["r_near"], s * 2 + 2)
                nc.gpsimd.tensor_tensor(out=sums[:], in0=sums[:], in1=rsum[:], op=ALU.mult).then_inc(S["newton"], 1)
                link(1)
                nc.gpsimd.tensor_tensor(out=sums[:], in0=two[:, 0:1].to_broadcast([P, N]), in1=sums[:], op=ALU.subtract).then_inc(S["newton"], 1)
                link(2)
                nc.gpsimd.tensor_tensor(out=rsum[:], in0=rsum[:], in1=sums[:], op=ALU.mult).then_inc(S["newton"], 1)
                link(3)
                pool.wait_ge(S["ot_raw"], n_half(s, 1))
                nc.gpsimd.tensor_tensor(out=ot[:, pp, :], in0=ot[:, pp, :], in1=rsum[:], op=ALU.mult).then_inc(S["n_done"], 1)

            def body(b, first, last):
                for pp in range(2):
                    s = b * 2 + pp
                    for j in range(1, T):
                        if last and pp == 1:
                            continue
                        pool.wait_ge(S["p_ready"], n_unit(s, j, 1, 1))
                        if j == 1:
                            if not (first and pp == 0):
                                pool.wait_ge(S["l_full"], n_half(s - 1, 1))
                        else:
                            pool.wait_ge(S["sum_done"], s * (T - 1) + (j - 1))
                        nc.gpsimd.tensor_tensor(out=psums[:], in0=(probs[0] if j == 1 else psums)[:], in1=probs[j % RING][:],
                                                op=ALU.add).then_inc(S["sum_done"], 1)
                        if j == 3 and not (first and pp == 0):
                            normalise(s - 1, 1 - pp)
                    if last and pp == 1:
                        normalise(s - 1, 1 - pp)
                    if pp == 1:
                        pool.wait_ge(S["x_in"], b * 16 + 16)
                        nc.gpsimd.tensor_tensor(out=y[:], in0=y[:], in1=bias_row[:].rearrange("p (a d) -> p a d", a=1).to_broadcast([P, T, D]),
                                                op=ALU.add).then_inc(S["xb_done"], 1)

            drive(nc.gpsimd, body)


_OUT = ((8, 1024, 256), "float32")


def kernel(x, adj, L0_gnn_Wq, L0_gnn_Wk, L0_gnn_Wv, L0_gnn_Wo, L0_gnn_bo):
    import numpy as _np
    import concourse.bacc as _bacc
    from concourse import mybir as _mybir
    from concourse.bass_utils import run_bass_kernel_spmd as _run

    nc = _bacc.Bacc("TRN2", target_bir_lowering=False, num_devices=1)
    x, adj = _np.asarray(x), _np.asarray(adj)
    sent = {
        "xt": x.transpose(0, 2, 1), "x": x, "adj": adj, "adjt": adj.transpose(0, 2, 1),
        "wq": L0_gnn_Wq, "wk": L0_gnn_Wk, "wv": L0_gnn_Wv, "wo": L0_gnn_Wo, "bo": L0_gnn_bo,
    }
    arrays, args = {}, []
    for name, a in sent.items():
        a = _np.ascontiguousarray(a)
        arrays[f"in_{name}_dram"] = a
        args.append(nc.dram_tensor(f"in_{name}_dram", a.shape, _mybir.dt.from_np(a.dtype), kind="ExternalInput").ap())
    args.append(nc.dram_tensor("out_0_dram", _OUT[0], _mybir.dt.from_np(_np.dtype(_OUT[1])), kind="ExternalOutput").ap())
    masked_attention_residual_norm(nc, *args)
    r = _run(nc, [arrays], core_ids=[0])
    return r.results[0]["out_0_dram"]
```

```python
from contextlib import ExitStack

import concourse.bass as bass
from concourse import mybir

F32 = mybir.dt.float32
F32R = mybir.dt.float32r
BF16 = mybir.dt.bfloat16
U8 = mybir.dt.uint8
ALU = mybir.AluOpType
ACT = mybir.ActivationFunctionType
AX_X = mybir.AxisListType.X

P = 128
HALF = 512
BIG = 2.0 ** 100
EPS = 1e-5


def slot_plan(pp):
    plan = [[[] for _ in range(6)] for _ in range(8)]
    maxima = [("max", (i, h, f)) for i in range(8) for h in range(2) for f in range(2)]
    for s, places in MAXIMA:
        for at in places:
            plan[s][at].append(maxima.pop(0))
    assert not maxima
    for kind, idx, s, at in MORE[pp]:
        plan[s][at].append((kind, idx))
    return plan


CONVERT_SLOTS = [(4, 4, 6, 7), (1, 3, 7, 7)]
MAXIMA = [(1, (4, 5)), (2, (0, 1, 2, 3, 5)), (3, (0, 1, 2, 3, 4, 5)), (4, (1, 2, 3, 4, 5)),
          (5, (0, 1, 2, 3, 4, 5)), (6, (1, 2, 3, 4, 5)), (7, (1, 2, 4))]
MORE = [
    [("v", 3, 0, 4), ("l", 0, 2, 5), ("l", 1, 3, 0), ("prj", 0, 4, 0), ("prj", 1, 6, 0), ("prj", 2, 6, 0),
     ("prj", 3, 6, 0), ("o", 0, 7, 1), ("o", 1, 7, 1), ("mt", 0, 7, 5), ("mt", 1, 7, 5)],
    [("o", 2, 0, 0), ("o", 3, 0, 0), ("agg", 0, 0, 2), ("fin", 0, 1, 1), ("l", 0, 1, 4), ("l", 1, 2, 5),
     ("v", 0, 3, 0), ("prj", 0, 4, 0), ("prj", 1, 6, 0), ("prj", 2, 6, 0), ("prj", 3, 6, 0), ("v", 1, 6, 2),
     ("v", 2, 7, 4), ("mt", 0, 7, 5), ("mt", 1, 7, 5)],
]
LAST_SUMS = {3: (1,), 4: (2, 3), 5: (4,), 6: (5,), 7: (6,)}
PROLOGUE_MORE = {0: [("v", 0, 1), ("conv", 1, False)], 1: [("v", 1, 1), ("conv", 2, False)],
                 2: [("v", 2, 1), ("conv", 3, False)], 4: [("prj", 0, 1)], 5: [("prj", 1, 1), ("conv", 0, True)],
                 6: [("prj", 2, 1), ("conv", 1, True)], 7: [("prj", 3, 1)]}
STAGED_MAXIMA = 5
PARTS = [["a0", "s00", "s01", "s10", "a1", "s11"], ["s00", "s01", "s10", "a0", "a1", "s11"],
         ["s00", "s01", "a0", "s10", "s11", "a1"], ["s00", "s01", "a0", "s10", "s11", "a1"],
         ["s00", "a0", "s01", "s10", "s11", "a1"], ["s00", "s01", "a0", "s10", "s11", "a1"],
         ["s00", "s01", "a0", "s10", "s11", "a1"], ["s00", "s01", "s10", "s11", "a0", "a1"]]
PLANS = [slot_plan(0), slot_plan(1)]
MASKED_BY_PE = [[(0, 1)], [(0, 0), (0, 1), (1, 1)], [(0, 1)], [(0, 0), (1, 1)], [(0, 1), (1, 1)], [(0, 1), (1, 1)],
                [(0, 1)], [(0, 1), (1, 1)]]
MASKED_BY_DVE = [(j, h, f) for j in range(8) for h in range(2) for f in range(2) if (h, f) not in MASKED_BY_PE[j]]


class AuxBanks:

    def __init__(self, banks):
        self.banks, self.n, self.held_by = banks, 0, [None] * len(banks)

    def next(self):
        self.n += 1
        return self.banks[(self.n - 1) % len(self.banks)]

    def take(self, item):
        k = self.n % len(self.banks)
        before, self.held_by[k] = self.held_by[k], item
        return self.next(), before

    def enter_loop(self, b):
        self.held_by = [(kind, idx, b - 1, pp) for kind, idx, _, pp in self.held_by]


def masked_attention_residual_norm(nc, xt, x, adj, adjt, wq, wk, wv, wo, bo, out):
    B, N, D = x.shape
    H = 4
    DH = D // H
    PAIRS = H // 2
    T = N // P
    KT = D // P
    SCALE = DH ** -0.5
    RING = 4
    assert T == 8 and KT == 2 and DH == 64 and PAIRS == 2 and N == 2 * HALF

    xt_v = xt.rearrange("b (k p) n -> b p k n", p=P)
    x_v = x.rearrange("b (t p) d -> b p t d", p=P)
    out_v = out.rearrange("b (t p) d -> b p t d", p=P)
    adj_v = adj.rearrange("b (c t p) n -> b c p t n", p=P, t=2)
    adjt_v = adjt.rearrange("b (c t p) n -> b c p t n", p=P, t=2)
    w_v = [w.rearrange("(k p) n -> p k n", p=P) for w in (wq, wk, wv, wo)]

    with ExitStack() as ctx:
        def sb(name, shape, dt=F32):
            return ctx.enter_context(nc.sbuf_tensor(name, shape, dt))

        def psum(name, shape):
            return ctx.enter_context(nc.psum_tensor(name, shape, F32))

        def sem(name):
            return ctx.enter_context(nc.semaphore(name))

        w_sb = [sb(f"w{n}", [P, KT, D]) for n in ("q", "k", "v", "o")]
        bias_row = sb("bias_row", [P, D])
        ident = sb("ident", [P, P])
        ident0 = sb("ident0", [P, P])
        ident_bf = sb("ident_bf", [P, P], BF16)
        ones = sb("ones", [P, DH])
        eps = sb("eps", [P, 1])
        two = sb("two", [P, 1])
        xt_sb = sb("xt_sb", [P, KT, N])
        adj_u8 = [sb(f"adj_u8_{i}", [P, 2, N], U8) for i in range(2)]
        mask_n = sb("mask_n", [P, T, N], BF16)
        mask_t = sb("mask_t", [P, T, N], BF16)
        qk1 = [sb(f"qk1_{i}", [P, 2, 2, N], F32R) for i in range(2)]
        qk2 = [sb(f"qk2_{i}", [P, 2, 2, N], F32R) for i in range(2)]
        q1 = [t[:, 0] for t in qk1]
        k1 = [t[:, 1] for t in qk1]
        q2 = [t[:, 0] for t in qk2]
        k2 = [t[:, 1] for t in qk2]
        staged = sb("staged", [P, 4, N], F32R)
        hi = [staged[:, 0], staged[:, 2]]
        lo = [staged[:, 1], staged[:, 3]]
        v_sb = sb("v_sb", [P, T, D])
        probs = [sb(f"probs{i}", [P, 2, N]) for i in range(RING)]
        psums = sb("psums", [P, 2, N])
        ot = sb("ot", [P, PAIRS, N])
        sums = sb("sums", [P, N])
        rsum = sb("rsum", [P, N])
        y = sb("y", [P, T, D])
        mx = sb("mx", [P, T, 2, 2])
        m = sb("m", [P, T, 2])
        stats = sb("stats", [P, T, 6])
        mv = sb("mv", [P, T, 2])
        near = sb("near", [P, T])
        var = sb("var", [P, T])
        newton_t = sb("newton_t", [P, T])
        rstd = sb("rstd", [P, T])

        st = [[psum(f"st{h}{f}", [P, HALF]) for f in range(2)] for h in range(2)]
        ot_ps = psum("ot_ps", [P, 2, HALF])
        aux = [psum(f"aux{i}", [P, HALF]) for i in range(2)]

        all_banks = aux + st[0] + st[1]

        names = ("wq_in wk_in wv_in wo_in bias_in xt_half_in xt_in adj_in0 adj_in1 x_in out_st op_in w_pool apart ident_set const_set sel_set "
                 "st_full pv_done max_full mt_full prj_full v_full l_full o_full "
                 "masked max_red m_done lo_done r_done n_done half_done l_copied r_near newton y_sum y_stat y_aggr y_rstd y_done "
                 "p_ready hi_done mrow_done v_ready ot_raw conv near_done sum_done xb_done")
        S = {n: sem(n) for n in names.split()}
        w_in = [S["wq_in"], S["wk_in"], S["wv_in"], S["wo_in"]]
        adj_in = [S["adj_in0"], S["adj_in1"]]

        def n_unit(s, j, h, f):
            return s * 32 + (4 * j + 2 * h + f + 1)

        def n_masked(s, j, h, f):
            return s * len(MASKED_BY_DVE) + (MASKED_BY_DVE.index((j, h, f)) + 1)

        def n_tile(s, j):
            return s * T + (j + 1)

        def n_max(s, i, h, f):
            return s * 32 + (4 * i + 2 * h + f + 1)

        def n_half(s, f):
            return s * 2 + (f + 1)

        def n_row(s, f):
            return s * 4 + (2 * f + 2)

        def n_prj(s, k):
            return s * 4 + (k + 1)

        def n_four(b, c):
            return b * 4 + (c + 1)

        def n_conv(b, c, transposed):
            return b * 8 + (4 * transposed + c + 1)

        def reader_of(kind, idx, b, pp):
            s = b * 2 + pp
            if kind == "max":
                return S["max_red"], n_max(s + 1, *idx)
            if kind == "mt":
                return S["mrow_done"], n_row(s + 1, idx)
            if kind == "prj":
                return S["lo_done"], n_prj(s + 2, idx)
            if kind == "v":
                return S["v_ready"], n_four(b + 1 if pp else b, idx)
            if kind == "l":
                return S["l_copied"], n_half(s - 1, idx)
            return S["y_sum"], n_four(b - 1, idx)

        def present(kind, idx, b, pp, first, last):
            if kind in ("max", "mt"):
                return not (last and pp == 1)
            if kind == "prj":
                return not last
            if kind == "v":
                return not (last and pp == 1)
            if kind == "l":
                return not (first and pp == 0)
            return not first

        def drive(engine, body, banks=None):
            body(0, True, False)
            with engine.Fori(1, B - 1) as b:
                if banks is not None:
                    banks.enter_loop(b)
                body(b, False, False)
            if banks is not None:
                banks.enter_loop(B - 1)
            body(B - 1, False, True)

        def wait_apart(engine, semaphore, value):
            engine.wait_ge(semaphore, value)
            if not isinstance(value, int):
                engine.sem_inc(S["apart"], 1)

        prologue = [("prj", k, 0) for k in range(4)] + [("conv", 0, False)]
        for i in range(T):
            prologue += [("max", (i, h, f), 1) for h in range(2) for f in range(2)]
            prologue += PROLOGUE_MORE.get(i, [])
        prologue += [("mt", f, 1) for f in range(2)]

        block = ctx.enter_context(nc.Block())

        @block.sync
        def _(sp):
            def load_adj(b, c, transposed):
                g = 4 * transposed + c
                if not (isinstance(b, int) and b == 0 and g < 2):
                    wait_apart(sp, S["conv"], b * 8 + (g - 1))
                src = (adjt_v if transposed else adj_v)[b, c]
                sp.dma_start(adj_u8[g % 2][:], src).then_inc(adj_in[g % 2], 16)

            def load_ops(s, par):
                sp.wait_ge(S["hi_done"], n_prj(s, 3))
                sp.wait_ge(S["lo_done"], n_prj(s, 3))
                if not isinstance(s, int) or s >= 2:
                    sp.wait_ge(S["st_full"], n_unit(s - 2, T - 1, 1, 1))
                for h in range(2):
                    own, other = (slice(h * DH, (h + 1) * DH), slice((1 - h) * DH, (2 - h) * DH))
                    for src, dst in (
                        (staged[own, 0::2], qk1[par][own, :, h]),
                        (staged[own, 1:3], qk1[par][other, :, h]),
                        (staged[own, 0::3], qk2[par][own, :, h]),
                    ):
                        sp.dma_start(dst.bitcast(F32), src.bitcast(F32)).then_inc(S["op_in"], 16)

            def store(b):
                for f in range(2):
                    wait_apart(sp, S["y_done"], b * T + (T // 2) * (f + 1))
                    h = slice(f * T // 2, (f + 1) * T // 2)
                    sp.dma_start(out_v[b][:, h], y[:, h]).then_inc(S["out_st"], 16)

            def body(b, first, last):
                if not last:
                    wait_apart(sp, S["v_full"], n_four(b, 3))
                    sp.dma_start(xt_sb[:], xt_v[b + 1]).then_inc(S["xt_in"], 16)
                    for c in range(4):
                        load_adj(b + 1, c, False)
                    load_ops(b * 2 + 2, 0)
                    for c in range(2):
                        load_adj(b + 1, c, True)
                if not first:
                    store(b - 1)
                    wait_apart(sp, S["out_st"], b * 32)
                sp.dma_start(y[:], x_v[b]).then_inc(S["x_in"], 16)
                if not last:
                    for c in range(2, 4):
                        load_adj(b + 1, c, True)
                    load_ops(b * 2 + 3, 1)

            sp.dma_start(w_sb[0][:], w_v[0]).then_inc(w_in[0], 16)
            sp.dma_start(xt_sb[:, :, 0:HALF], xt_v[0][:, :, 0:HALF]).then_inc(S["xt_half_in"], 16)
            sp.dma_start(xt_sb[:, :, HALF:N], xt_v[0][:, :, HALF:N]).then_inc(S["xt_in"], 16)
            for n in range(1, 4):
                sp.dma_start(w_sb[n][:], w_v[n]).then_inc(w_in[n], 16)
            sp.dma_start(bias_row[:], bo.rearrange("(a d) -> a d", a=1).to_broadcast([P, D])).then_inc(S["bias_in"], 16)
            load_adj(0, 0, False)
            load_adj(0, 1, False)
            load_adj(0, 2, False)
            load_ops(0, 0)
            load_adj(0, 3, False)
            for c in range(4):
                load_adj(0, c, True)
            load_ops(1, 1)
            drive(nc.sync, body)
            store(B - 1)
            sp.wait_ge(S["out_st"], B * 32)

        @block.tensor
        def _(pe):
            banks = AuxBanks(all_banks)

            def scores(s, pp, j, h, f):
                if h == 0 and f == 0 and j == 0:
                    pe.wait_ge(S["mrow_done"], n_row(s, 1))
                if not (isinstance(s, int) and s == 0 and j == 0):
                    pe.wait_ge(S["p_ready"], n_unit(s, j, h, f) - 4)
                js, fs = slice(j * P, (j + 1) * P), slice(f * HALF, (f + 1) * HALF)
                by_dve = (j, h, f) in MASKED_BY_DVE
                nc.tensor.matmul(st[h][f][:], k1[pp][:, h, js], q1[pp][:, h, fs], start=True, stop=False)
                done = nc.tensor.matmul(st[h][f][:], k2[pp][:, h, js], q2[pp][:, h, fs], start=False, stop=by_dve)
                if not by_dve:
                    done = nc.tensor.matmul(st[h][f][:], ident_bf[:], mask_t[:, j, fs], start=False, stop=True)
                done.then_inc(S["st_full"], 1)

            def attend(s, pp, j, f):
                pe.wait_ge(S["p_ready"], n_unit(s, j, 1, f))
                if f == 0:
                    if j % 2 == 0 and pp == 0:
                        pe.wait_ge(S["v_ready"], s * 2 + (j // 2 + 1))
                    if j == 0 and not (isinstance(s, int) and s == 0):
                        pe.wait_ge(S["ot_raw"], n_half(s - 1, 1))
                fs = slice(f * HALF, (f + 1) * HALF)
                for h in range(2):
                    c = (pp * 2 + h) * DH
                    last = nc.tensor.matmul(ot_ps[h * DH:(h + 1) * DH, f], v_sb[:, j, c:c + DH],
                                            probs[j % RING][:, h, fs], start=(j == 0), stop=(j == T - 1))
                if f == 1:
                    last.then_inc(S["pv_done"], 1)

            def item(kind, idx, b, pp):
                s = b * 2 + pp
                after = isinstance(b, int) and b == B
                bank, before = banks.take((kind, idx, b, pp))
                if before is not None:
                    pe.wait_ge(*reader_of(*before))
                if kind == "max" and isinstance(b, int) and b < 0 and idx[0] < STAGED_MAXIMA:
                    i, h, f = idx
                    own = slice(h * DH, (h + 1) * DH)
                    if i == 0 and h == 0 and f == 0:
                        pe.wait_ge(S["hi_done"], n_prj(0, 3))
                        pe.wait_ge(S["lo_done"], n_prj(0, 3))
                    for part in (hi, lo):
                        last = nc.tensor.matmul(bank[:], part[0][own, i * P:(i + 1) * P], hi[1][own, f * HALF:(f + 1) * HALF],
                                                start=(part is hi), stop=(part is lo))
                    last.then_inc(S["max_full"], 1)
                elif kind == "max":
                    i, h, f = idx
                    par = (pp + 1) % 2
                    if (i == 0 or isinstance(b, int) and b < 0) and h == 0 and f == 0:
                        pe.wait_ge(S["op_in"], s * 96 + 192)
                    nc.tensor.matmul(bank[:], q1[par][:, h, i * P:(i + 1) * P], k1[par][:, h, f * HALF:(f + 1) * HALF],
                                     start=True, stop=True).then_inc(S["max_full"], 1)
                elif kind == "mt":
                    if idx == 0:
                        if isinstance(s, int) and s < 0:
                            pe.wait_ge(S["ident_set"], 1)
                        pe.wait_ge(S["m_done"], s + 2)
                    for t in range(4):
                        last = nc.tensor.transpose(bank[0:2, t * P:(t + 1) * P], m[:, 4 * idx + t, :], ident[:])
                    last.then_inc(S["mt_full"], 1)
                elif kind == "prj":
                    which, f = idx // 2, idx % 2
                    par = pp
                    if idx == 0 and par == 0 and not (isinstance(b, int) and b < 0):
                        pe.wait_ge(S["xt_in"], b * 16 + 32)
                    for k in range(KT):
                        last = nc.tensor.matmul(bank[:], w_sb[which][:, k, par * P:(par + 1) * P],
                                                xt_sb[:, k, f * HALF:(f + 1) * HALF], start=(k == 0), stop=(k == KT - 1))
                    last.then_inc(S["prj_full"], 1)
                elif kind == "v":
                    for t in range(2):
                        j = 2 * idx + t
                        for k in range(KT):
                            last = nc.tensor.matmul(bank[:, t * D:(t + 1) * D], xt_sb[:, k, j * P:(j + 1) * P],
                                                    w_sb[2][:, k, :], start=(k == 0), stop=(k == KT - 1))
                    last.then_inc(S["v_full"], 1)
                elif kind == "l":
                    if idx == 0:
                        pe.wait_ge(S["sum_done"], (s - 1) * (T - 1) + (T - 1 - after))
                    for h in range(2):
                        qs = slice(idx * HALF, (idx + 1) * HALF)
                        last = nc.tensor.matmul(bank[h * DH:(h + 1) * DH, :], ones[:], psums[:, h, qs], start=True, stop=not after)
                        if after:
                            last = nc.tensor.matmul(bank[h * DH:(h + 1) * DH, :], ones[:], probs[(T - 1) % RING][:, h, qs],
                                                    start=False, stop=True)
                    last.then_inc(S["l_full"], 1)
                else:
                    if after:
                        pe.wait_ge(S["n_done"], 2 * B - 1 + idx // 2)
                        pe.wait_ge(S["half_done"], 2)
                    elif idx == 0:
                        pe.wait_ge(S["n_done"], b * 2)
                    for t in range(2):
                        i = 2 * idx + t
                        for k in range(KT):
                            last = nc.tensor.matmul(bank[:, t * D:(t + 1) * D], ot[:, k, i * P:(i + 1) * P],
                                                    w_sb[3][:, k, :], start=(k == 0), stop=(k == KT - 1))
                    last.then_inc(S["o_full"], 1)

            def body(b, first, last):
                for pp in range(2):
                    s = b * 2 + pp
                    for j in range(T):
                        for g, part in enumerate(PARTS[j]):
                            if part == "s00" and pp == 0 and j % 2 == 0:
                                pe.wait_ge(S["conv"], n_conv(b, j // 2, True))
                            if part[0] == "s":
                                scores(s, pp, j, int(part[1]), int(part[2]))
                            elif j > 0:
                                attend(s, pp, j - 1, int(part[1]))
                            elif not (first and pp == 0):
                                attend(s - 1, 1 - pp, T - 1, int(part[1]))
                            for kind, idx in PLANS[pp][j][g]:
                                if kind not in ("agg", "fin") and present(kind, idx, b, pp, first, last):
                                    item(kind, idx, b, pp)

            pe.wait_ge(S["wq_in"], 16)
            pe.wait_ge(S["xt_half_in"], 16)
            for kind, idx, pp in prologue:
                if kind == "conv":
                    continue
                if pp == 0 and idx == 1:
                    pe.wait_ge(S["xt_in"], 16)
                if pp == 0 and idx == 2:
                    pe.wait_ge(S["wk_in"], 16)
                if kind == "v" and idx == 0:
                    pe.wait_ge(S["wv_in"], 16)
                item(kind, idx, -1, pp)
            pe.wait_ge(S["max_red"], n_max(0, T - 1, 1, 1))
            pe.wait_ge(S["v_ready"], 3)
            pe.wait_ge(S["lo_done"], n_prj(1, 3))
            pe.wait_ge(S["mrow_done"], n_row(0, 1))
            pe.wait_ge(S["wo_in"], 16)
            pe.wait_ge(S["const_set"], 3)
            banks = AuxBanks(aux)
            pe.wait_ge(S["sel_set"], 9)
            drive(nc.tensor, body, banks)
            attend(2 * B - 1, 1, T - 1, 0)
            attend(2 * B - 1, 1, T - 1, 1)
            for f in range(2):
                item("l", f, B, 0)
            banks = AuxBanks(st[0] + st[1])
            for c in range(4):
                item("o", c, B, 0)

        @block.vector
        def _(dve):
            banks = AuxBanks(all_banks)

            def mask(s, j, h, f):
                dve.wait_ge(S["st_full"], n_unit(s, j, h, f))
                nc.vector.tensor_tensor(out=st[h][f][:], in0=st[h][f][:], in1=mask_t[:, j, f * HALF:(f + 1) * HALF],
                                        op=ALU.add).then_inc(S["masked"], 1)

            def sum_tile(j):
                dve.wait_ge(S["p_ready"], n_unit(2 * B - 1, j, 1, 1))
                if j == 1:
                    dve.wait_ge(S["l_full"], n_half(2 * B - 2, 1))
                else:
                    dve.wait_ge(S["sum_done"], (2 * B - 1) * (T - 1) + (j - 1))
                nc.vector.tensor_tensor(out=psums[:], in0=(probs[0] if j == 1 else psums)[:], in1=probs[j % RING][:],
                                        op=ALU.add).then_inc(S["sum_done"], 1)

            def norm(b, c):
                for t in range(2 * c, 2 * c + 2):
                    nc.vector.bn_stats(stats[:, t, :], y[:, t, :]).then_inc(S["y_stat"], 1)

            def aggregate(b, tiles):
                wait_apart(dve, S["y_stat"], b * T + tiles.stop)
                for t in range(T)[tiles]:
                    nc.vector.bn_aggr(mv[:, t, :], stats[:, t, :]).then_inc(S["y_aggr"], 1)

            def finish(tiles, count):
                def link(n):
                    dve.wait_ge(S["y_rstd"], (count - 1) * 5 + n)

                v, r, t = var[:, tiles], near[:, tiles], newton_t[:, tiles]
                dve.wait_ge(S["near_done"], count * 2)
                nc.vector.tensor_tensor(out=t, in0=r, in1=r, op=ALU.mult).then_inc(S["y_rstd"], 1)
                nc.vector.tensor_scalar(v, mv[:, tiles, 1], EPS, None, ALU.add).then_inc(S["y_rstd"], 1)
                link(2)
                nc.vector.tensor_tensor(out=t, in0=t, in1=v, op=ALU.mult).then_inc(S["y_rstd"], 1)
                link(3)
                nc.vector.tensor_scalar(t, t, -0.5, 1.5, ALU.mult, ALU.add).then_inc(S["y_rstd"], 1)
                link(4)
                nc.vector.tensor_tensor(out=rstd[:, tiles], in0=t, in1=r, op=ALU.mult).then_inc(S["y_rstd"], 1)
                link(5)
                for t in range(T)[tiles]:
                    nc.vector.tensor_scalar(y[:, t, :], y[:, t, :], mv[:, t, 0:1], rstd[:, t:t + 1],
                                            ALU.subtract, ALU.mult).then_inc(S["y_done"], 1)

            def item(kind, idx, b, pp):
                s = b * 2 + pp
                bank = banks.next()
                if kind == "max":
                    i, h, f = idx
                    if h == 0 and f == 0 and i % 2 == 0:
                        dve.wait_ge(S["conv"], n_conv(b + pp, i // 2, False))
                    if i == 0 and h == 0 and f == 0 and not (isinstance(s, int) and s < 0):
                        dve.wait_ge(S["m_done"], s + 1)
                    wait_apart(dve, S["max_full"], n_max(s + 1, i, h, f))
                    nc.vector.tensor_tensor_reduce(
                        out=bank[:], in0=bank[:], in1=mask_n[:, i, f * HALF:(f + 1) * HALF], scale=1.0,
                        scalar=-3.0e38, op0=ALU.add, op1=ALU.max, accum_out=mx[:, i, h, f:f + 1]).then_inc(S["max_red"], 1)
                    if i == T - 1 and h == 1 and f == 1:
                        dve.wait_ge(S["max_red"], n_max(s + 1, i, h, f))
                        if not (isinstance(s, int) and s < 0):
                            dve.wait_ge(S["mt_full"], n_half(s, 1))
                        nc.vector.tensor_reduce(m[:], mx[:], AX_X, ALU.max).then_inc(S["m_done"], 1)
                elif kind == "prj":
                    which, f = idx // 2, idx % 2
                    fs = slice(f * HALF, (f + 1) * HALF)
                    if idx == 0 and not (isinstance(s, int) and s < -1):
                        dve.wait_ge(S["op_in"], s * 96 + 192)
                    dve.wait_ge(S["hi_done"], n_prj(s + 2, idx))
                    nc.vector.tensor_tensor(out=lo[which][:, fs], in0=bank[:], in1=hi[which][:, fs].bitcast(F32),
                                            op=ALU.subtract).then_inc(S["lo_done"], 1)
                elif kind == "o":
                    if idx == 0:
                        dve.wait_ge(S["xb_done"], b)
                    dve.wait_ge(S["o_full"], n_four(b - 1, idx))
                    ys = y[:, 2 * idx:2 * idx + 2, :]
                    nc.vector.tensor_tensor(out=ys, in0=bank[:].rearrange("p (t d) -> p t d", t=2), in1=ys,
                                            op=ALU.add).then_inc(S["y_sum"], 1)
                    dve.wait_ge(S["y_sum"], n_four(b - 1, idx))
                    norm(b - 1, idx)

            def body(b, first, last):
                for pp in range(2):
                    s = b * 2 + pp
                    for j in range(T):
                        for g, part in enumerate(PARTS[j]):
                            if part == "s00" and pp == 0 and j % 2 == 0:
                                dve.wait_ge(S["conv"], n_conv(b, j // 2, True))
                            if part[0] == "s" and (j, int(part[1]), int(part[2])) in MASKED_BY_DVE:
                                mask(s, j, int(part[1]), int(part[2]))
                            if part == "s11" and last and pp == 1:
                                for tile in LAST_SUMS.get(j, ()):
                                    sum_tile(tile)
                            for kind, idx in PLANS[pp][j][g]:
                                if not present(kind, idx, b, pp, first, last):
                                    continue
                                if kind == "agg":
                                    aggregate(b - 1, slice(0, T))
                                elif kind == "fin":
                                    finish(slice(0, T), b)
                                else:
                                    item(kind, idx, b, pp)

            dve.wait_ge(S["ident_set"], 1)
            nc.vector.tensor_copy(ident_bf[:], ident[:]).then_inc(S["sel_set"], 1)
            for par in range(2):
                nc.vector.memset(q2[par][DH:P, 0, :].bitcast(F32), 0.0).then_inc(S["sel_set"], 1)
                nc.vector.memset(q2[par][0:DH, 1, :].bitcast(F32), 0.0).then_inc(S["sel_set"], 1)
                nc.vector.tensor_copy(k2[par][DH:P, 0, :], ident[DH:P, DH:DH + 1].to_broadcast([DH, N])).then_inc(S["sel_set"], 1)
                nc.vector.tensor_copy(k2[par][0:DH, 1, :], ident[0:DH, 1:2].to_broadcast([DH, N])).then_inc(S["sel_set"], 1)
            for kind, idx, pp in prologue:
                if kind != "conv":
                    item(kind, idx, -1, pp)
            banks = AuxBanks(aux)
            drive(nc.vector, body)
            bank, fs = banks.next(), slice(0, HALF)
            dve.wait_ge(S["l_full"], n_half(2 * B - 1, 0))
            dve.wait_ge(S["n_done"], 2 * B - 1)
            nc.vector.reciprocal(rsum[:, fs], bank[:]).then_inc(S["half_done"], 1)
            dve.wait_ge(S["half_done"], 1)
            dve.wait_ge(S["ot_raw"], n_half(2 * B - 1, 0))
            nc.vector.tensor_tensor(out=ot[:, 1, fs], in0=ot[:, 1, fs], in1=rsum[:, fs], op=ALU.mult).then_inc(S["half_done"], 1)
            banks = AuxBanks(st[0] + st[1])
            early, late = slice(0, T // 2), slice(T // 2, T)
            item("o", 0, B, 0)
            item("o", 1, B, 0)
            aggregate(B - 1, early)
            item("o", 2, B, 0)
            item("o", 3, B, 0)
            aggregate(B - 1, late)
            finish(early, B)
            finish(late, B + 1)

        @block.scalar
        def _(act):
            banks = AuxBanks(all_banks)

            def convert(b, c, transposed):
                g = 4 * transposed + c
                act.wait_ge(adj_in[g % 2], b * 64 + 16 * (g // 2 + 1))
                if not (isinstance(b, int) and b == 0):
                    if transposed:
                        act.wait_ge(S["st_full"], n_unit(b * 2 - 1, 2 * c + 1, 1, 1))
                        act.wait_ge(S["masked"], n_masked(b * 2 - 1, *[u for u in MASKED_BY_DVE if u[0] <= 2 * c + 1][-1]))
                    else:
                        act.wait_ge(S["max_red"], n_max(b * 2 - 1, 2 * c + 1, 1, 1))
                dst = (mask_t if transposed else mask_n)[:, 2 * c:2 * c + 2, :]
                nc.scalar.activation(dst, adj_u8[g % 2][:], ACT.Copy, bias=-BIG, scale=BIG).then_inc(S["conv"], 1)

            def exp(s, pp, j, h, f):
                if h == 0 and f == 0 and not (isinstance(s, int) and s == 0 and j < RING):
                    act.wait_ge(S["pv_done"], s * T + (j - RING + 1))
                    if j < RING:
                        act.wait_ge(S["sum_done"], s * (T - 1) + min(j - RING + T, T - 1) - (T - 1))
                    else:
                        act.wait_ge(S["sum_done"], s * (T - 1) + max(j - RING, 1))
                if (j, h, f) in MASKED_BY_DVE:
                    act.wait_ge(S["masked"], n_masked(s, j, h, f))
                else:
                    act.wait_ge(S["st_full"], n_unit(s, j, h, f))
                nc.scalar.activation(probs[j % RING][:, h, f * HALF:(f + 1) * HALF], st[h][f][:],
                                     ACT.Exp, scale=SCALE).then_inc(S["p_ready"], 1)

            def near_reciprocal(s, queries):
                nc.scalar.activation(rsum[:, queries], sums[:, queries], ACT.Ln).then_inc(S["r_near"], 1)
                act.wait_ge(S["r_near"], s * 2 + 1)
                nc.scalar.activation(rsum[:, queries], rsum[:, queries], ACT.Exp, scale=-1.0).then_inc(S["r_near"], 1)

            def item(kind, idx, b, pp):
                s = b * 2 + pp
                bank = banks.next()
                if kind == "mt":
                    act.wait_ge(S["mt_full"], n_half(s + 1, idx))
                    if idx == 0 and isinstance(s, int) and s < 0:
                        act.wait_ge(S["sel_set"], 9)
                    par = (pp + 1) % 2
                    fs = slice(idx * HALF, (idx + 1) * HALF)
                    nc.scalar.mul(q2[par][DH:DH + 2, 0, fs], bank[0:2, :], -1.0).then_inc(S["mrow_done"], 1)
                    nc.scalar.mul(q2[par][0:2, 1, fs], bank[0:2, :], -1.0).then_inc(S["mrow_done"], 1)
                elif kind == "prj":
                    which, f = idx // 2, idx % 2
                    if idx == 0 and not (isinstance(s, int) and s < -1):
                        act.wait_ge(S["op_in"], s * 96 + 192)
                    if idx == 0 and isinstance(s, int) and s == -1:
                        act.wait_ge(S["max_full"], n_max(0, STAGED_MAXIMA - 1, 1, 1))
                    act.wait_ge(S["prj_full"], n_prj(s + 2, idx))
                    nc.scalar.copy(hi[which][:, f * HALF:(f + 1) * HALF], bank[:]).then_inc(S["hi_done"], 1)
                elif kind == "l":
                    act.wait_ge(S["l_full"], n_half(s - 1, idx))
                    if idx == 0 and not (isinstance(s, int) and s == 1):
                        act.wait_ge(S["n_done"], s - 1)
                    nc.scalar.copy(sums[:, idx * HALF:(idx + 1) * HALF], bank[:]).then_inc(S["l_copied"], 1)
                    if idx == 1:
                        act.wait_ge(S["l_copied"], n_half(s - 1, 1))
                        near_reciprocal(s - 1, slice(0, N))
                elif kind == "v":
                    bb = b + 1 if pp else b
                    act.wait_ge(S["v_full"], n_four(bb, idx))
                    if not (isinstance(bb, int) and bb == 0):
                        act.wait_ge(S["pv_done"], n_tile(bb * 2 - 1, 2 * idx + 1))
                    nc.scalar.copy(v_sb[:, 2 * idx:2 * idx + 2, :], bank[:].rearrange("p (t d) -> p t d", t=2)).then_inc(S["v_ready"], 1)

            def deviation(b, tiles, count):
                act.wait_ge(S["y_aggr"], b * T + tiles.stop)
                if not (isinstance(count, int) and count in (1, B + 1)):
                    act.wait_ge(S["y_rstd"], (count - 1) * 5)
                nc.scalar.activation(near[:, tiles], mv[:, tiles, 1], ACT.Ln, bias=eps[:, 0:1], scale=1.0).then_inc(S["near_done"], 1)
                act.wait_ge(S["near_done"], count * 2 - 1)
                nc.scalar.activation(near[:, tiles], near[:, tiles], ACT.Exp, scale=-0.5).then_inc(S["near_done"], 1)

            def body(b, first, last):
                for pp in range(2):
                    s = b * 2 + pp
                    for j in range(T):
                        for g, part in enumerate(PARTS[j]):
                            if part[0] == "s":
                                exp(s, pp, j, int(part[1]), int(part[2]))
                            if part == "a1" and j == 0 and not (first and pp == 0):
                                raw_step(b, pp, first)
                            for kind, idx in PLANS[pp][j][g]:
                                if not present(kind, idx, b, pp, first, last):
                                    continue
                                if kind == "fin":
                                    continue
                                if kind == "agg":
                                    deviation(b - 1, slice(0, T), b)
                                else:
                                    item(kind, idx, b, pp)
                        if not last:
                            for c in range(4):
                                if CONVERT_SLOTS[pp][c] == j:
                                    convert(b + 1, c, pp == 1)

            def raw_step(b, pp, first):
                s = b * 2 + pp - 1
                q = 1 - pp
                act.wait_ge(S["pv_done"], n_tile(s, T - 1))
                if q == 0 and not first:
                    act.wait_ge(S["o_full"], b * 4)
                for f in range(2):
                    nc.scalar.copy(ot[:, q, f * HALF:(f + 1) * HALF], ot_ps[:, f]).then_inc(S["ot_raw"], 1)

            nc.scalar.preload_act_table_set("natural_log_exp_and_others")
            act.wait_ge(S["const_set"], 3)
            for kind, idx, pp in prologue:
                if kind == "conv":
                    convert(0, idx, pp)
                else:
                    item(kind, idx, -1, pp)
            convert(0, 2, True)
            convert(0, 3, True)
            banks = AuxBanks(aux)
            drive(nc.scalar, body)
            raw_step(B, 0, False)
            banks.next()
            bank, late = banks.next(), slice(HALF, N)
            act.wait_ge(S["l_full"], n_half(2 * B - 1, 1))
            act.wait_ge(S["n_done"], 2 * B - 1)
            nc.scalar.copy(sums[:, late], bank[:]).then_inc(S["l_copied"], 1)
            act.wait_ge(S["l_copied"], n_half(2 * B - 1, 0))
            near_reciprocal(2 * B - 1, late)
            deviation(B - 1, slice(0, T // 2), B)
            deviation(B - 1, slice(T // 2, T), B + 1)

        @block.gpsimd
        def _(pool):
            nc.gpsimd.memset(ones[:], 1.0).then_inc(S["const_set"], 1)
            nc.gpsimd.memset(eps[:], EPS).then_inc(S["const_set"], 1)
            nc.gpsimd.memset(two[:], 2.0).then_inc(S["const_set"], 1)
            nc.gpsimd.memset(ident0[:], 1.0).then_inc(S["w_pool"], 1)
            pool.wait_ge(S["w_pool"], 1)
            nc.gpsimd.affine_select(out=ident[:], in_=ident0[:], compare_op=ALU.is_equal, fill=0.0, base=0,
                                    pattern=[[-1, P]], channel_multiplier=1).then_inc(S["ident_set"], 1)
            pool.wait_ge(S["bias_in"], 16)

            def normalise(s, pp, queries=slice(0, N)):
                def link(n):
                    pool.wait_ge(S["newton"], s * 3 + n)

                l, r, o = sums[:, queries], rsum[:, queries], ot[:, pp, queries]
                width = queries.stop - queries.start
                pool.wait_ge(S["r_near"], s * 2 + 2)
                nc.gpsimd.tensor_tensor(out=l, in0=l, in1=r, op=ALU.mult).then_inc(S["newton"], 1)
                link(1)
                nc.gpsimd.tensor_tensor(out=l, in0=two[:, 0:1].to_broadcast([P, width]), in1=l, op=ALU.subtract).then_inc(S["newton"], 1)
                link(2)
                nc.gpsimd.tensor_tensor(out=r, in0=r, in1=l, op=ALU.mult).then_inc(S["newton"], 1)
                link(3)
                pool.wait_ge(S["ot_raw"], n_half(s, 1))
                nc.gpsimd.tensor_tensor(out=o, in0=o, in1=r, op=ALU.mult).then_inc(S["n_done"], 1)

            def body(b, first, last):
                for pp in range(2):
                    s = b * 2 + pp
                    for j in range(1, T):
                        if last and pp == 1:
                            continue
                        pool.wait_ge(S["p_ready"], n_unit(s, j, 1, 1))
                        if j == 1:
                            if not (first and pp == 0):
                                pool.wait_ge(S["l_full"], n_half(s - 1, 1))
                        else:
                            pool.wait_ge(S["sum_done"], s * (T - 1) + (j - 1))
                        nc.gpsimd.tensor_tensor(out=psums[:], in0=(probs[0] if j == 1 else psums)[:], in1=probs[j % RING][:],
                                                op=ALU.add).then_inc(S["sum_done"], 1)
                        if j == 3 and not (first and pp == 0):
                            normalise(s - 1, 1 - pp)
                    if last and pp == 1:
                        normalise(s - 1, 1 - pp)
                    if pp == 1:
                        pool.wait_ge(S["x_in"], b * 16 + 16)
                        nc.gpsimd.tensor_tensor(out=y[:], in0=y[:], in1=bias_row[:].rearrange("p (a d) -> p a d", a=1).to_broadcast([P, T, D]),
                                                op=ALU.add).then_inc(S["xb_done"], 1)

            drive(nc.gpsimd, body)
            normalise(2 * B - 1, 1, slice(HALF, N))


_OUT = ((8, 1024, 256), "float32")


def kernel(x, adj, L0_gnn_Wq, L0_gnn_Wk, L0_gnn_Wv, L0_gnn_Wo, L0_gnn_bo):
    import numpy as _np
    import concourse.bacc as _bacc
    from concourse import mybir as _mybir
    from concourse.bass_utils import run_bass_kernel_spmd as _run

    nc = _bacc.Bacc("TRN2", target_bir_lowering=False, num_devices=1)
    x, adj = _np.asarray(x), _np.asarray(adj)
    sent = {
        "xt": x.transpose(0, 2, 1), "x": x, "adj": adj, "adjt": adj.transpose(0, 2, 1),
        "wq": L0_gnn_Wq, "wk": L0_gnn_Wk, "wv": L0_gnn_Wv, "wo": L0_gnn_Wo, "bo": L0_gnn_bo,
    }
    arrays, args = {}, []
    for name, a in sent.items():
        a = _np.ascontiguousarray(a)
        arrays[f"in_{name}_dram"] = a
        args.append(nc.dram_tensor(f"in_{name}_dram", a.shape, _mybir.dt.from_np(a.dtype), kind="ExternalInput").ap())
    args.append(nc.dram_tensor("out_0_dram", _OUT[0], _mybir.dt.from_np(_np.dtype(_OUT[1])), kind="ExternalOutput").ap())
    masked_attention_residual_norm(nc, *args)
    r = _run(nc, [arrays], core_ids=[0])
    return r.results[0]["out_0_dram"]
```
